# Optimizing a Trainium2 kernel written in Bass

```python
import numpy as np
import jax
import jax.numpy as jnp

def _softmax(x, axis=-1):
    return jax.nn.softmax(x, axis=axis)

def _gelu(x):
    return jax.nn.gelu(x, approximate=True)

def _silu(x):
    return jax.nn.silu(x)

def _sigmoid(x):
    return jax.nn.sigmoid(x)

def _layernorm(x, axis=-1, eps=1e-05):
    m = jnp.mean(x, axis=axis, keepdims=True)
    v = jnp.var(x, axis=axis, keepdims=True)
    return (x - m) / jnp.sqrt(v + eps)

def _scatter_add(tgt, idx, src, axis=0):
    return tgt.at[idx].add(src)

def _segment_sum(src, seg, n):
    return jax.ops.segment_sum(src, seg, n)
kernel_name = 'mk_gnn_resnorm_d4_gnn_r8_55eafd'

def setup_inputs(seed: int=0):
    np.random.seed(seed)
    _w = jnp.asarray

    def _rec_inputs():
        import jax
        import jax.numpy as jnp
        _gk = jax.random.key(seed)
        x = -0.0003713 + 1 * jax.random.normal(jax.random.fold_in(_gk, 1), (6250, 256), jnp.float32)
        src = jax.random.randint(jax.random.fold_in(_gk, 2), (100000,), 0, 6250, jnp.int32)
        dst = jax.random.randint(jax.random.fold_in(_gk, 3), (100000,), 0, 6250, jnp.int32)
        _o = jnp.argsort(dst, stable=True)
        src = src[_o]
        dst = dst[_o]
        edge_attr_64 = 0.000312547 + 1.00004 * jax.random.normal(jax.random.fold_in(_gk, 12), (100000, 64), jnp.float32)
        edge_type_16 = jax.random.randint(jax.random.fold_in(_gk, 14), (100000,), 0, 16, jnp.int32)
        edge_weight1 = jax.random.uniform(jax.random.fold_in(_gk, 15), (100000, 1), jnp.float32, 0.0, 1)
        return (x, src, dst, edge_attr_64, edge_type_16, edge_weight1)
    x, src, dst, edge_attr_64, edge_type_16, edge_weight1 = _rec_inputs()

    def _L0_gnn_setup():
        import jax, jax.numpy as jnp
        import numpy as np
        N_NODES = 6250
        N_EDGES = 100000
        NUM_RELS = 16
        FEAT = 256
        OUT = 256
        key = jax.random.key(seed)
        ks = jax.random.split(key, 7)
        h = jax.random.normal(ks[0], (N_NODES, FEAT), dtype=jnp.float32)
        norm = jax.random.uniform(ks[1], (N_EDGES, 1), dtype=jnp.float32)
        weight = jax.random.normal(ks[2], (NUM_RELS, FEAT, OUT), dtype=jnp.float32) * 0.05
        gate_weight = jax.random.normal(ks[3], (NUM_RELS, FEAT, 1), dtype=jnp.float32) * 0.05
        src = jax.random.randint(ks[4], (N_EDGES,), 0, N_NODES)
        dst = jax.random.randint(ks[5], (N_EDGES,), 0, N_NODES)
        rel_type = jax.random.randint(ks[6], (N_EDGES,), 0, NUM_RELS)
        return {'h': h, 'norm': norm, 'weight': weight, 'gate_weight': gate_weight, 'src': src, 'dst': dst, 'rel_type': rel_type}
    _L0_gnn_all = _L0_gnn_setup()
    _L0_gnn_in = {k: v for k, v in _L0_gnn_all.items() if k in ('weight', 'gate_weight')}
    del _L0_gnn_all

    def _L1_gnn_setup():
        import jax, jax.numpy as jnp
        import numpy as np
        N_NODES = 12500
        N_EDGES = 200000
        D_IN = 256
        D_OUT = 256
        key = jax.random.key(seed)
        k1, k2, k3, k4 = jax.random.split(key, 4)
        x = jax.random.normal(k1, (N_NODES, D_IN), dtype=jnp.float32)
        edge_index = jax.random.randint(k2, (2, N_EDGES), 0, N_NODES, dtype=jnp.int64)
        W = jax.random.normal(k3, (D_OUT, D_IN), dtype=jnp.float32) * (1.0 / np.sqrt(D_IN))
        b = jax.random.normal(k4, (D_OUT,), dtype=jnp.float32) * 0.01
        return {'x': x, 'edge_index': edge_index, 'W': W, 'b': b}
    _L1_gnn_all = _L1_gnn_setup()
    _L1_gnn_in = {k: v for k, v in _L1_gnn_all.items() if k in ('W', 'b')}
    del _L1_gnn_all

    def _L2_gnn_setup():
        import jax, jax.numpy as jnp
        import numpy as np
        N, E, H, DE = (1250, 31250, 256, 64)
        EPS = 1e-05

        def _lin_init(k, fan_in, shape):
            s = 1.0 / np.sqrt(fan_in)
            return jax.random.uniform(k, shape, jnp.float32, -s, s)
        key = jax.random.key(seed)
        ks = jax.random.split(key, 12)
        x = jax.random.normal(ks[0], (N, H), jnp.float32)
        edge_index = jax.random.randint(ks[1], (2, E), 0, N)
        edge_attr = jax.random.normal(ks[2], (E, DE), jnp.float32)
        d_in = H + DE
        W1 = _lin_init(ks[3], d_in, (d_in, H))
        b1 = _lin_init(ks[4], d_in, (H,))
        W2 = _lin_init(ks[5], H, (H, H))
        b2 = _lin_init(ks[6], H, (H,))
        Wg = _lin_init(ks[7], d_in, (d_in, H))
        bg = _lin_init(ks[8], d_in, (H,))
        gamma = jnp.ones((H,), jnp.float32)
        beta = jnp.zeros((H,), jnp.float32)
        return {'x': x, 'edge_index': edge_index, 'edge_attr': edge_attr, 'W1': W1, 'b1': b1, 'W2': W2, 'b2': b2, 'Wg': Wg, 'bg': bg, 'gamma': gamma, 'beta': beta}
    _L2_gnn_all = _L2_gnn_setup()
    _L2_gnn_in = {k: v for k, v in _L2_gnn_all.items() if k in ('W1', 'b1', 'W2', 'b2', 'Wg', 'bg', 'gamma', 'beta')}
    del _L2_gnn_all

    def _L3_gnn_setup():
        import jax, jax.numpy as jnp
        import numpy as np
        N = 6250
        E = 200000
        D = 256
        H = 256
        EPS = 1e-05

        def _gnn_layer(x, row, col, W, b, g, beta):
            n = x.shape[0]
            neigh = x[col]
            agg = jax.ops.segment_sum(neigh, row, num_segments=n)
            deg = jax.ops.segment_sum(jnp.ones((row.shape[0],), x.dtype), row, num_segments=n)
            deg = jnp.maximum(deg, 1.0)[:, None]
            h = (x + agg / deg) @ W.T + b
            mu = jnp.mean(h, axis=-1, keepdims=True)
            var = jnp.mean(jnp.square(h - mu), axis=-1, keepdims=True)
            hn = (h - mu) * jax.lax.rsqrt(var + EPS) * g + beta
            return jax.nn.silu(hn)
        key = jax.random.key(seed)
        ks = jax.random.split(key, 12)
        x = jax.random.normal(ks[0], (N, D), dtype=jnp.float32)
        edge_index = jax.random.randint(ks[1], (2, E), 0, N, dtype=jnp.int32)
        s0 = 1.0 / np.sqrt(D)
        s1 = 1.0 / np.sqrt(H)
        W0 = jax.random.uniform(ks[2], (H, D), jnp.float32, -s0, s0)
        b0 = jax.random.uniform(ks[3], (H,), jnp.float32, -s0, s0)
        g0 = jnp.ones((H,), jnp.float32)
        beta0 = jnp.zeros((H,), jnp.float32)
        W1 = jax.random.uniform(ks[4], (H, H), jnp.float32, -s1, s1)
        b1 = jax.random.uniform(ks[5], (H,), jnp.float32, -s1, s1)
        g1 = jnp.ones((H,), jnp.float32)
        beta1 = jnp.zeros((H,), jnp.float32)
        return {'x': x, 'edge_index': edge_index, 'W0': W0, 'b0': b0, 'g0': g0, 'beta0': beta0, 'W1': W1, 'b1': b1, 'g1': g1, 'beta1': beta1}
    _L3_gnn_all = _L3_gnn_setup()
    _L3_gnn_in = {k: v for k, v in _L3_gnn_all.items() if k in ('W0', 'b0', 'g0', 'beta0', 'W1', 'b1', 'g1', 'beta1')}
    del _L3_gnn_all
    return {'x': x, 'src': src, 'dst': dst, 'edge_attr_64': edge_attr_64, 'edge_type_16': edge_type_16, 'edge_weight1': edge_weight1, 'L0_gnn_weight': _L0_gnn_in['weight'], 'L0_gnn_gate_weight': _L0_gnn_in['gate_weight'], 'L1_gnn_W': _L1_gnn_in['W'], 'L1_gnn_b': _L1_gnn_in['b'], 'L2_gnn_W1': _L2_gnn_in['W1'], 'L2_gnn_b1': _L2_gnn_in['b1'], 'L2_gnn_W2': _L2_gnn_in['W2'], 'L2_gnn_b2': _L2_gnn_in['b2'], 'L2_gnn_Wg': _L2_gnn_in['Wg'], 'L2_gnn_bg': _L2_gnn_in['bg'], 'L2_gnn_gamma': _L2_gnn_in['gamma'], 'L2_gnn_beta': _L2_gnn_in['beta'], 'L3_gnn_W0': _L3_gnn_in['W0'], 'L3_gnn_b0': _L3_gnn_in['b0'], 'L3_gnn_g0': _L3_gnn_in['g0'], 'L3_gnn_beta0': _L3_gnn_in['beta0'], 'L3_gnn_W1': _L3_gnn_in['W1'], 'L3_gnn_b1': _L3_gnn_in['b1'], 'L3_gnn_g1': _L3_gnn_in['g1'], 'L3_gnn_beta1': _L3_gnn_in['beta1']}

def reference(x, src, dst, edge_attr_64, edge_type_16, edge_weight1, L0_gnn_weight, L0_gnn_gate_weight, L1_gnn_W, L1_gnn_b, L2_gnn_W1, L2_gnn_b1, L2_gnn_W2, L2_gnn_b2, L2_gnn_Wg, L2_gnn_bg, L2_gnn_gamma, L2_gnn_beta, L3_gnn_W0, L3_gnn_b0, L3_gnn_g0, L3_gnn_beta0, L3_gnn_W1, L3_gnn_b1, L3_gnn_g1, L3_gnn_beta1):
    import jax
    import jax.numpy as jnp

    def _L0_gnn_ref(h, norm, weight, gate_weight, src, dst, rel_type):
        import jax, jax.numpy as jnp
        import numpy as np
        N_NODES = 6250
        N_EDGES = 100000
        NUM_RELS = 16
        FEAT = 256
        OUT = 256
        n_nodes = h.shape[0]
        all_msg = jnp.einsum('nf,rfo->rno', h, weight)
        msg = all_msg[rel_type, src] * norm
        all_gate = jnp.einsum('nf,rf->rn', h, gate_weight[..., 0])
        gate = jax.nn.sigmoid(all_gate[rel_type, src])[:, None]
        msg = msg * gate
        agg = jax.ops.segment_sum(msg, dst, num_segments=n_nodes)
        return jax.nn.relu(agg)

    def _L1_gnn_ref(x, edge_index, W, b):
        import jax, jax.numpy as jnp
        import numpy as np
        N_NODES = 12500
        N_EDGES = 200000
        D_IN = 256
        D_OUT = 256
        h = jnp.einsum('nd,od->no', x, W) + b
        row, col = (edge_index[0], edge_index[1])
        msgs = h[col]
        out = jax.ops.segment_sum(msgs, row, num_segments=h.shape[0])
        return out

    def _L2_gnn_ref(x, edge_index, edge_attr, W1, b1, W2, b2, Wg, bg, gamma, beta):
        import jax, jax.numpy as jnp
        import numpy as np
        N, E, H, DE = (1250, 31250, 256, 64)
        EPS = 1e-05

        def _lin_init(k, fan_in, shape):
            s = 1.0 / np.sqrt(fan_in)
            return jax.random.uniform(k, shape, jnp.float32, -s, s)
        src, dst = (edge_index[0], edge_index[1])
        ei = jnp.concatenate([x[src], edge_attr], axis=-1)
        core = jnp.maximum(ei @ W1 + b1, 0.0) @ W2 + b2
        gate = jax.nn.sigmoid(ei @ Wg + bg)
        msg = gate * core
        agg = jax.ops.segment_sum(msg, dst, num_segments=x.shape[0])
        out = agg + x
        mu = jnp.mean(out, axis=-1, keepdims=True)
        var = jnp.var(out, axis=-1, keepdims=True)
        out = (out - mu) * jax.lax.rsqrt(var + EPS) * gamma + beta
        return out

    def _L3_gnn_ref(x, edge_index, W0, b0, g0, beta0, W1, b1, g1, beta1):
        import jax, jax.numpy as jnp
        import numpy as np
        N = 6250
        E = 200000
        D = 256
        H = 256
        EPS = 1e-05

        def _gnn_layer(x, row, col, W, b, g, beta):
            n = x.shape[0]
            neigh = x[col]
            agg = jax.ops.segment_sum(neigh, row, num_segments=n)
            deg = jax.ops.segment_sum(jnp.ones((row.shape[0],), x.dtype), row, num_segments=n)
            deg = jnp.maximum(deg, 1.0)[:, None]
            h = (x + agg / deg) @ W.T + b
            mu = jnp.mean(h, axis=-1, keepdims=True)
            var = jnp.mean(jnp.square(h - mu), axis=-1, keepdims=True)
            hn = (h - mu) * jax.lax.rsqrt(var + EPS) * g + beta
            return jax.nn.silu(hn)
        row, col = (edge_index[0], edge_index[1])
        x = _gnn_layer(x, row, col, W0, b0, g0, beta0)
        x = _gnn_layer(x, row, col, W1, b1, g1, beta1)
        return x
    edge_index = jnp.stack([src, dst])
    x = _layernorm(x + _L0_gnn_ref(x, edge_weight1, L0_gnn_weight, L0_gnn_gate_weight, src, dst, edge_type_16), axis=-1)
    x = _layernorm(x + _L1_gnn_ref(x, edge_index, L1_gnn_W, L1_gnn_b), axis=-1)
    x = _layernorm(x + _L2_gnn_ref(x, edge_index, edge_attr_64, L2_gnn_W1, L2_gnn_b1, L2_gnn_W2, L2_gnn_b2, L2_gnn_Wg, L2_gnn_bg, L2_gnn_gamma, L2_gnn_beta), axis=-1)
    x = _layernorm(x + _L3_gnn_ref(x, edge_index, L3_gnn_W0, L3_gnn_b0, L3_gnn_g0, L3_gnn_beta0, L3_gnn_W1, L3_gnn_b1, L3_gnn_g1, L3_gnn_beta1), axis=-1)
    return x

_drawn_inputs = setup_inputs


def setup_inputs(seed=0):
    import zlib

    import numpy as np

    out = dict(_drawn_inputs(seed))
    spreads = {'L2_gnn_gamma': (1.0, 0.2),
     'L2_gnn_beta': (0.0, 0.1),
     'L3_gnn_g0': (1.0, 0.2),
     'L3_gnn_beta0': (0.0, 0.1),
     'L3_gnn_g1': (1.0, 0.2),
     'L3_gnn_beta1': (0.0, 0.1)}
    factors = {'L2_gnn_bg': 6.641}
    for name, (base, spread) in spreads.items():
        noise = np.random.default_rng([zlib.crc32(name.encode()), seed]).standard_normal(out[name].shape)
        drawn = base * np.exp(spread * noise) if base else spread * noise
        out[name] = jnp.asarray(drawn.astype(out[name].dtype))
    for name, factor in factors.items():
        out[name] = (out[name] * factor).astype(out[name].dtype)
    return out
```

```python
from contextlib import ExitStack

import concourse.bass as bass
from concourse import mybir

ALU = mybir.AluOpType
ACT = mybir.ActivationFunctionType
F32 = mybir.dt.float32
I32 = mybir.dt.int32
R32 = mybir.dt.float32r

P = 128
N, D = 6250, 256
E, DE, R = 100000, 64, 16
KC = D // P
NB = 50
FULL = N // P
TAIL = N - FULL * P
EPP = 125
EPT = E // EPP
USED = FULL + 1
TILES = 832
SLOTS = TILES * P
U = 8
BODY = 2 * U
TURNS = TILES // BODY
SC = 16
SCHUNKS = EPT // SC
RW = 6
SW = 3
LATE = 16
AW = D + 1
EPS = 1e-5
TB = 7
assert TILES * P >= E + USED * (P - 1) and TILES % BODY == 0 and EPT % (2 * SC) == 0


class Chain:

    def __init__(self, eng, sem):
        self.eng, self.sem, self.base, self.n = eng, sem, 0, 0

    def step(self, ins):
        ins.then_inc(self.sem, 1)
        self.n += 1

    def wait(self):
        self.eng.wait_ge(self.sem, self.base + self.n)

    def enter(self, i, per):
        self.outer, self.per = self.base + self.n, per
        self.base, self.n = self.outer + i * per, 0

    def leave(self, turns):
        assert self.n == self.per, (self.n, self.per)
        self.base, self.n = self.outer + turns * self.per, 0


def program(nc, x, src, dst, edge_attr, edge_type, edge_weight, w_rel, w_gate, w_l1, b_l1,
            w1, b1, w2, b2, wg, bg, gamma, beta, w_a, b_a, g_a, be_a, w_b, b_b, g_b, be_b, out):
    ctx = ExitStack()
    with ctx:
        def sb(name, shape, dt=F32):
            return ctx.enter_context(nc.sbuf_tensor(name, shape, dt))

        def sem(name):
            return ctx.enter_context(nc.semaphore(name))

        t_rel = nc.dram_tensor("t_rel", (NB * P * R, D), F32).ap()
        t_h = nc.dram_tensor("t_h", (NB * P, D), F32).ap()
        t_pg = nc.dram_tensor("t_pg", (NB * P, 2 * D), F32).ap()
        t_x3 = nc.dram_tensor("t_x3", (NB * P, D), F32).ap()
        t_y1 = nc.dram_tensor("t_y1", (NB * P, D), F32).ap()
        r_dst = nc.dram_tensor("r_dst", (SLOTS, RW), I32).ap()
        r_src = nc.dram_tensor("r_src", (SLOTS, SW), I32).ap()
        d_tb = nc.dram_tensor("d_tb", (2, TB * P), I32).ap()

        X = sb("X", [P, NB, D])
        acc = sb("acc", [P, NB, AW])
        accf = acc[:, :, :].rearrange("p b w -> p (b w)")
        wrel = accf[:, 0:KC * R * D].rearrange("p (c n) -> p c n", c=KC)
        o = KC * R * D
        blk = {k: accf[0:EPP, o + n * EPT:o + (n + 1) * EPT] for n, k in enumerate(("dst", "src"))}
        ind, run, slot = (accf[0:EPP, o + n * EPT:o + (n + 1) * EPT] for n in (2, 3, 4))
        arena = sb("arena", [P, 4096])
        stage = arena[:, :].rearrange("p (s n) -> p s n", s=2)
        raw = arena[0:EPP, 0:4 * EPT].rearrange("p (k t) -> p k t", k=4)
        G = arena[:, :].rearrange("p (s n) -> p s n", s=U)
        early = sb("early", [P, EPT * RW])
        recd = early[0:EPP, :].bitcast(I32).rearrange("p (t w) -> p t w", w=RW)
        recs = sb("recs", [EPP, EPT, SW], I32)
        scat = sb("scat", [EPP, 2, SC * RW], I32)
        tmpl = sb("tmpl", [P, U * RW], I32)
        tmpls = sb("tmpls", [P, U * SW], I32)
        rec = sb("rec", [P, 2, U * RW], I32)
        lane = sb("lane", [P, P])
        ident = sb("ident", [P, P])
        ones = sb("ones", [P, P])
        tri = sb("tri", [P, P])
        tcol = sb("tcol", [P, TB])
        zero = sb("zero", [P, 1])
        epsc = sb("epsc", [P, 1])
        cnt = sb("cnt", [P, 2, P])
        blks = sb("blks", [P, 8, 64])
        blki = sb("blki", [P, 64], I32)
        tbf = sb("tbf", [P, 2, TB])
        tbi = sb("tbi", [P, 2, TB], I32)
        tbrow = sb("tbrow", [1, 2, TB * P], I32)
        tj = sb("tj", [P, 64])
        wgate = sb("wgate", [P, KC, R])
        wl1 = sb("wl1", [P, KC, D])
        wpg = sb("wpg", [P, KC, 2 * D])
        weh, wel = sb("weh", [P, 2 * D], R32), sb("wel", [P, 2 * D], R32)
        w2h, w2l = sb("w2h", [P, KC, D], R32), sb("w2l", [P, KC, D], R32)
        wab = sb("wab", [P, 2, KC, D])
        bpg = sb("bpg", [P, 2 * D])
        b2w = sb("b2w", [64, D])
        b2h = sb("b2h", [64, D], R32)
        ones_r = sb("ones_r", [64, P], R32)
        rows = {}
        for name in ("b_l1", "gamma", "beta", "b_a", "g_a", "be_a", "b_b", "g_b", "be_b"):
            rows[name] = sb("row_" + name, [P, D])
        gate = sb("gate", [P, 2, R])
        xs = sb("xs", [P, 2, D])
        xT = sb("xT", [P, 2, KC, P])
        ts = sb("ts", [P, 2, D])
        st = sb("st", [P, 2, 2 * D])
        stats = sb("stats", [P, NB, 6])
        mean = sb("mean", [P, NB])
        rstd = sb("rstd", [P, NB])
        lt = sb("lt", [P, 2, NB])
        rdeg = sb("rdeg", [P, NB])
        onehot = early[:, 0:U * P].rearrange("p (s n) -> p s n", s=U)
        sg = early[:, 2 * U * P:2 * U * P + 2 * D].rearrange("p (s n) -> p s n", s=2)
        attr = early[:, U * P:U * (P + DE)].rearrange("p (s n) -> p s n", s=U)
        attrT = sb("attrT", [P, 2, P], R32)
        HTh, HTl = sb("HTh", [P, 2, KC, P], R32), sb("HTl", [P, 2, KC, P], R32)
        gs, msg = xs, ts

        ps = [ctx.enter_context(nc.psum_tensor(f"ps{i}", [P, 512], F32)) for i in range(8)]

        s_ld = {k: sem("ld_" + k) for k in ("edges", "x", "wrel", "wgate", "parts", "late")}
        xpad = sem("xpad")
        consts = sem("consts")
        tmpl_ready, prefilled = sem("tmpl_ready"), sem("prefilled")
        v_sem, a_sem = sem("v_chain"), sem("a_chain")
        raw_used = sem("raw_used")
        counted, based, slots_ready = sem("counted"), sem("based"), sem("slots_ready")
        tb_ready, tb_stored, tb_back = sem("tb_ready"), sem("tb_stored"), sem("tb_back")
        scat_in = [sem(f"scat_in{i}") for i in range(2)]
        scattered = [sem(f"scattered{i}") for i in range(2)]
        pool_ok = sem("pool_ok")
        act_ok = sem("act_ok")
        dve_ok, pe_ok = sem("dve_ok"), sem("pe_ok")
        q = {k: sem("q_" + k) for k in ("xs", "xt", "xtc", "pg", "pr", "gate", "ev", "st0", "st1")}
        acc_clear = sem("acc_clear")
        b2_clear = sem("b2_clear")
        ones_in = sem("ones_in")
        rec_in = [sem(f"rec_in{i}") for i in range(2)]
        gathered = [sem(f"gathered{i}") for i in range(U)]
        attr_in = [sem(f"attr_in{i}") for i in range(U)]
        hot = [sem(f"hot{L}") for L in range(5)]
        summed = [sem(f"summed{L}") for L in range(5)]
        done = [sem(f"done{L}") for L in range(5)]
        e = {k: sem("e_" + k) for k in ("at", "atc", "atl", "ht", "relu", "htl", "gp", "gs", "sig", "core", "msg")}
        n = [{k: sem(f"n{L}_{k}") for k in ("var", "std", "xs", "xsc", "tp", "tpc", "mm", "st", "sto0", "sto1",
                                            "ts", "sg", "ys", "accok")} for L in range(5)]
        x3_in = [sem(f"x3_in{i}") for i in range(2)]
        x3_used, out_ready = sem("x3_used"), sem("out_ready")

        block = ctx.enter_context(nc.Block())

        HALF = {0: 0, 1: 1, 2: 0, 3: 1, 4: 1}
        VIEW = [r_dst.rearrange("(p t) w -> p (t w)", p=P), r_src.rearrange("(p t) w -> p (t w)", p=P)]
        WORDS = [RW, SW]

        def X_(b):
            return X[:, bass.ds(b, 1), :].rearrange("p a w -> p (a w)")

        def acc_(b, w=D):
            return acc[:, bass.ds(b, 1), 0:w].rearrange("p a w -> p (a w)")

        @block.sync
        def _(sp):
            def load(name, dst_ap, src_ap):
                sp.dma_start(dst_ap, src_ap).then_inc(s_ld[name], 16)

            for L in range(5):
                sp.sem_inc(done[L], BODY)
                for k, v in (("xsc", 2), ("tp", 2), ("tpc", 2), ("mm", 2), ("st", 2), ("ys", 2), ("sto0", 16), ("sto1", 16)):
                    sp.sem_inc(n[L][k], v)
            for k, v in (("xt", 2), ("xtc", 2), ("gate", 1), ("ev", 8), ("st0", 16), ("st1", 16)):
                sp.sem_inc(q[k], v)
            for k, v in (("atl", 1), ("gp", 2), ("core", 2), ("msg", 2), ("htl", 2), ("gs", 2), ("sig", 2)):
                sp.sem_inc(e[k], v)
            sp.sem_inc(x3_used, 2)

            for k, a in enumerate((src, dst, edge_type)):
                load("edges", raw[:, k, :].bitcast(I32), a.rearrange("(p t) -> p t", p=EPP))
            load("edges", raw[:, 3, :], edge_weight.rearrange("(p t) a -> p (t a)", p=EPP))
            load("x", X[:, 0:FULL, :], x[0:FULL * P, :].rearrange("(b p) f -> p b f", p=P))
            sp.wait_ge(xpad, 1)
            load("x", X[0:TAIL, FULL, :], x[FULL * P:N, :])
            load("wgate", wgate[:, :, :], w_gate.rearrange("(c p) r -> p c r", p=P))
            for c in range(KC):
                load("wrel", wrel[:, c, :].rearrange("p (r o) -> p r o", r=R),
                     w_rel[:, c * P:(c + 1) * P, :].rearrange("r p o -> p r o"))
            sp.wait_ge(tmpl_ready, 2)
            for view, t, w in ((VIEW[0], tmpl, RW), (VIEW[1], tmpls, SW)):
                for k in range(4):
                    n_rep = TILES // U // 4
                    sp.dma_start(view[:, k * n_rep * U * w:(k + 1) * n_rep * U * w].rearrange("p (a w) -> p a w", a=n_rep),
                                 t[:, :].unsqueeze(1).broadcast_to([P, n_rep, U * w])).then_inc(prefilled, 16)
            for h in range(2):
                for k, w in enumerate((w1, wg)):
                    load("parts", st[h * DE:(h + 1) * DE, 0, k * D:(k + 1) * D], w[D:D + DE, :])
            load("parts", st[:, 1, :].rearrange("p (c o) -> p c o", c=KC), w2.rearrange("(c p) o -> p c o", p=P))
            sp.wait_ge(b2_clear, 1)
            for r in (0, 32):
                load("parts", b2w[r:r + 1, :], b2.rearrange("(a d) -> a d", a=1))
            for a, b in ((wl1[:, :, :], w_l1), (wab[:, 0], w_a), (wab[:, 1], w_b),
                         (wpg[:, :, 0:D], w1[0:D, :]), (wpg[:, :, D:2 * D], wg[0:D, :])):
                load("late", a, b.rearrange("(c p) o -> p c o", p=P))
            load("late", bpg[:, 0:D], b1.partition_broadcast(P))
            load("late", bpg[:, D:2 * D], bg.partition_broadcast(P))
            for name, a in (("b_l1", b_l1), ("gamma", gamma), ("beta", beta), ("b_a", b_a), ("g_a", g_a),
                            ("be_a", be_a), ("b_b", b_b), ("g_b", g_b), ("be_b", be_b)):
                load("late", rows[name][:, :], a.partition_broadcast(P))

            def scatter_chunks(k):
                sp.wait_ge(slots_ready, k + 1)
                rw = WORDS[k]
                big = (recd, recs)[k][:, :, :].rearrange("p t w -> p (t w)")
                base = k * (SCHUNKS // 2)
                for par in range(2):
                    if k:
                        sp.wait_ge(scattered[par], 16 * SC * base)
                    sp.dma_start(scat[:, par, 0:SC * rw], big[:, par * SC * rw:(par + 1) * SC * rw])\
                      .then_inc(scat_in[par], 16)
                with sp.Fori(1, SCHUNKS // 2) as c:
                    for par in range(2):
                        sp.wait_ge(scattered[par], (c + base) * (16 * SC))
                        sp.dma_start(scat[:, par, 0:SC * rw], big[:, bass.ds((c * 2 + par) * (SC * rw), SC * rw)])\
                          .then_inc(scat_in[par], 16)

            def block_rows(k):
                sp.wait_ge(tb_ready, k + 1)
                with nc.allow_non_contiguous_dma(reason="832 small words"):
                    sp.dma_start(d_tb[k, :].rearrange("(j p) -> p j", p=P), tbi[:, k, :]).then_inc(tb_stored, 16)
                sp.wait_ge(tb_stored, 16 * (k + 1))
                sp.dma_start(tbrow[:, k, :], d_tb[k:k + 1, :]).then_inc(tb_back, 16)

            def record_chunks(L):
                k = HALF[L]
                if L < 2:
                    for par in range(2):
                        sp.wait_ge(scattered[par], 16 * SC * (SCHUNKS // 2) * (k + 1))
                w = U * WORDS[k]
                with sp.Fori(0, TURNS) as c:
                    for par in range(2):
                        sp.wait_ge(done[L], c * BODY + par * U + U)
                        sp.dma_start(rec[:, par, 0:w], VIEW[k][:, bass.ds((c * 2 + par) * w, w)])\
                          .then_inc(rec_in[par], 16)

            def store_blocks(L, table, buf, ready, credits):
                with sp.Fori(0, NB // 2) as c:
                    for par in range(2):
                        sp.wait_ge(ready, c * 2 + par + (1 + credits))
                        sp.dma_start(table[bass.ds((c * 2 + par) * P, P), :], buf[par])\
                          .then_inc(n[L][f"sto{par}"], 16)

            scatter_chunks(0)
            block_rows(0)
            record_chunks(0)
            scatter_chunks(1)
            block_rows(1)
            store_blocks(0, t_h, [st[:, par, 0:D] for par in range(2)], n[0]["st"], 2)
            record_chunks(1)
            store_blocks(1, t_pg, [st[:, par, :] for par in range(2)], n[1]["st"], 2)
            record_chunks(2)
            store_blocks(2, t_x3, [xs[:, par, :] for par in range(2)], n[2]["xs"], 0)
            record_chunks(3)
            store_blocks(3, t_y1, [st[:, par, 0:D] for par in range(2)], n[3]["ys"], 2)
            record_chunks(4)
            sp.wait_ge(n[4]["mm"], NB + 2)
            with sp.Fori(0, NB // 2) as c:
                for par in range(2):
                    sp.wait_ge(x3_used, c * 2 + par + 1)
                    sp.dma_start(xs[:, par, :], t_x3[bass.ds((c * 2 + par) * P, P), :]).then_inc(x3_in[par], 16)
            with sp.Fori(0, FULL // 2) as c:
                for par in range(2):
                    sp.wait_ge(out_ready, c * 2 + par + 1)
                    sp.dma_start(out[bass.ds((c * 2 + par) * P, P), :], st[:, par, 0:D]).then_inc(n[4][f"sto{par}"], 16)
            sp.wait_ge(out_ready, FULL + 1)
            sp.dma_start(out[FULL * P:N, :], st[0:TAIL, 0, 0:D]).then_inc(n[4]["sto0"], 16)
            sp.wait_ge(n[4]["sto0"], 16 * (FULL // 2 + 1) + 16)
            sp.wait_ge(n[4]["sto1"], 16 * (FULL // 2) + 16)

        @block.gpsimd
        def _(pool):
            pool.memset(X[:, FULL:NB, :], 0.0).then_inc(xpad, 1)
            pool.memset(ones[:, :], 1.0).then_inc(consts, 1)
            pool.memset(ident[:, :], 0.0).then_inc(consts, 1)
            pool.memset(zero[:, :], 0.0).then_inc(consts, 1)
            pool.memset(epsc[:, :], EPS).then_inc(consts, 1)
            pool.iota(lane[:, :], [[1, P]], base=0, channel_multiplier=0,
                      allow_small_or_imprecise_dtypes=True).then_inc(consts, 1)
            pool.iota(tcol[:, :], [[P, TB]], base=0, channel_multiplier=1,
                      allow_small_or_imprecise_dtypes=True).then_inc(consts, 1)
            pool.iota(recd[:, :, 4], [[1, EPT]], base=0, channel_multiplier=EPT).then_inc(consts, 1)
            pool.memset(tmpl[:, :], 0).then_inc(consts, 1)
            pool.memset(tmpls[:, :], 0).then_inc(consts, 1)
            pool.memset(b2w[:, :], 0.0).then_inc(b2_clear, 1)
            pool.memset(ones_r[:, :].bitcast(F32), 1.0).then_inc(consts, 1)
            pool.wait_ge(consts, 10)
            pool.affine_select(out=ident[:, :], in_=ident[:, :], compare_op=ALU.not_equal, fill=1.0,
                               base=0, pattern=[[-1, P]], channel_multiplier=1).then_inc(consts, 1)
            pool.affine_select(out=tri[:, :], in_=ones[:, :], compare_op=ALU.is_gt, fill=0.0,
                               base=0, pattern=[[1, P]], channel_multiplier=-1).then_inc(consts, 1)
            pool.memset(tmpl[:, :].bitcast(F32).rearrange("p (t w) -> p t w", w=RW)[:, :, 2], -1.0).then_inc(tmpl_ready, 1)
            pool.memset(tmpls[:, :].bitcast(F32).rearrange("p (t w) -> p t w", w=SW)[:, :, 1], -1.0).then_inc(tmpl_ready, 1)

            def scatter(k):
                rw = WORDS[k]
                base = k * (SCHUNKS // 2)
                with pool.Fori(0, SCHUNKS // 2) as c:
                    for par in range(2):
                        pool.wait_ge(scat_in[par], (c + base) * 16 + 16)
                        pool.sem_inc(pool_ok, 1)
                        for j in range(SC):
                            r = scat[:, par, j * rw:(j + 1) * rw]
                            pool.indirect_dma_start(out=(r_dst, r_src)[k], in_=r, in_offset=None,
                                                    out_offset=bass.IndirectOffsetOnAxis(ap=r[:, rw - 1:rw], axis=0))\
                                .then_inc(scattered[par], 16)

            def gather(L, table, column, width, table_ready):
                k = HALF[L]
                rw = WORDS[k]
                table_ready()
                base_r, base_g = TURNS * L, 2 * TURNS * L
                with pool.Fori(0, TURNS) as c:
                    for j in range(BODY):
                        par, s, r = j // U, j % U, rec[:, j // U, (j % U) * rw:(j % U + 1) * rw]
                        if s == 0:
                            pool.wait_ge(rec_in[par], (c + base_r) * 16 + 16)
                            pool.sem_inc(pool_ok, 1)
                        pool.wait_ge(done[L], c * BODY + j + 1 + U)
                        pool.sem_inc(pool_ok, 1)
                        pool.indirect_dma_start(out=G[:, s, 0:width], out_offset=None, in_=table,
                                                in_offset=bass.IndirectOffsetOnAxis(ap=r[:, column:column + 1], axis=0))\
                            .then_inc(gathered[s], 16)
                        if L == 2:
                            pool.indirect_dma_start(out=attr[:, s, :], out_offset=None, in_=edge_attr,
                                                    in_offset=bass.IndirectOffsetOnAxis(ap=r[:, 4:5], axis=0))\
                                .then_inc(attr_in[s], 16)

            def clear(L):
                pool.wait_ge(n[L - 1]["accok"], 1)
                pool.memset(accf, 0.0).then_inc(acc_clear, 1)

            pool.wait_ge(prefilled, 16 * 8)
            scatter(0)
            pool.wait_ge(slots_ready, 2)
            pool.wait_ge(q["ev"], NB * R + 8)
            pool.memset(accf, 0.0).then_inc(acc_clear, 1)

            def rel_stored():
                for par in range(2):
                    pool.wait_ge(q[f"st{par}"], 16 * NB + 16)

            def stored(L):
                def wait():
                    for par in range(2):
                        pool.wait_ge(n[L][f"sto{par}"], 16 * (NB // 2) + 16)
                return wait

            gather(0, t_rel, 0, D, rel_stored)
            scatter(1)
            clear(1)
            pool.memset(G[:, :, D:D + 1], 1.0).then_inc(ones_in, 1)
            gather(1, t_h, 0, D, stored(0))
            clear(2)
            gather(2, t_pg, 1, 2 * D, stored(1))
            clear(3)
            gather(3, t_x3, 0, D, stored(2))
            clear(4)
            gather(4, t_y1, 0, D, stored(3))

        @block.vector
        def _(dve):
            ch = Chain(dve, v_sem)
            V = nc.vector

            dve.wait_ge(s_ld["edges"], 64)
            dve.wait_ge(consts, 12)
            ri = [raw[:, k, :].bitcast(I32) for k in range(4)]
            sc = ind.bitcast(I32)
            V.scalar_tensor_tensor(out=recd[:, :, 0], in0=ri[0], scalar=float(R), in1=ri[2],
                                   op0=ALU.mult, op1=ALU.add)
            V.tensor_copy(recd[:, :, 1], ri[0])
            V.tensor_copy(recd[:, :, 3].bitcast(F32), raw[:, 3, :])
            V.tensor_copy(recs[:, :, 0], ri[1])
            for key, r, to in ((1, ri[1], recd[:, :, 2]), (0, ri[0], recs[:, :, 1])):
                ch.step(V.tensor_scalar(sc, r, P - 1, None, ALU.bitwise_and))
                ch.wait()
                ch.step(V.tensor_copy(to.bitcast(F32), sc))
                ch.wait()
                ch.step(V.tensor_scalar(sc, r, 7, None, ALU.arith_shift_right))
                ch.wait()
                ch.step(V.tensor_copy(blk["dst" if key else "src"], sc))
                ch.wait()
            V.memset(tj[:, :], 0.0).then_inc(raw_used, 1)

            for k, key in enumerate(("dst", "src")):
                with dve.Fori(0, USED) as d:
                    ch.enter(d, 1)
                    ch.wait()
                    ch.step(V.tensor_scalar(ind, blk[key], lane[0:EPP, bass.ds(d, 1)], None, ALU.is_equal, ALU.add,
                                            accum_out=cnt[0:EPP, k, bass.ds(d, 1)]))
                    ch.leave(USED)
                ch.wait()
                dve.sem_inc(counted, 1)
            dve.wait_ge(based, 1)
            for k, key in enumerate(("dst", "src")):
                B = [blks[:, i, 0:USED] for i in range(8)]
                ch.step(V.tensor_scalar(B[0], ps[7][:, (2 * k + 1) * P:(2 * k + 1) * P + USED], float(P - 1), None, ALU.add))
                ch.step(V.tensor_copy(B[1], ps[7][:, 2 * k * P:2 * k * P + USED]))
                ch.wait()
                ch.step(V.tensor_copy(blki[:, 0:USED], B[0]))
                ch.wait()
                ch.step(V.tensor_scalar(blki[:, 0:USED], blki[:, 0:USED], 7, None, ALU.arith_shift_right))
                ch.wait()
                ch.step(V.tensor_copy(B[2], blki[:, 0:USED]))
                ch.wait()
                ch.step(V.tensor_tensor_scan(B[3], ones[:, 0:USED], B[2], 0.0, ALU.mult, ALU.add))
                ch.wait()
                ch.step(V.tensor_tensor(B[4], B[3], B[2], ALU.subtract))
                ch.wait()
                ch.step(V.scalar_tensor_tensor(out=B[5], in0=B[4], scalar=float(P), in1=B[1], op0=ALU.mult, op1=ALU.add))
                ch.wait()
                ch.step(V.tensor_scalar(B[6], B[5], -1.0, None, ALU.add))
                for j in range(TB):
                    ch.step(V.tensor_scalar(tj[:, 0:USED], B[3], tcol[:, j:j + 1], None, ALU.is_le, ALU.add,
                                            accum_out=tbf[:, k, j:j + 1]))
                    ch.wait()
                ch.step(V.tensor_scalar(tbf[:, k, :], tbf[:, k, :], float(USED - 1), None, ALU.min))
                ch.wait()
                ch.step(V.tensor_copy(tbi[:, k, :], tbf[:, k, :]))
                ch.wait()
                dve.sem_inc(tb_ready, 1)
                with dve.Fori(0, USED) as d:
                    ch.enter(d, 3)
                    ch.wait()
                    ch.step(V.tensor_scalar(ind, blk[key], lane[0:EPP, bass.ds(d, 1)], None, ALU.is_equal))
                    ch.wait()
                    ch.step(V.tensor_tensor_scan(run, ind, zero[0:EPP, 0:1].to_broadcast([EPP, EPT]),
                                                 blks[0:EPP, 6, bass.ds(d, 1)], ALU.add, ALU.add))
                    ch.wait()
                    dve.sem_inc(dve_ok, 1)
                    ch.step(V.copy_predicated(slot, ind.bitcast(I32), run))
                    ch.leave(USED)
                ch.wait()
                si, hi = ind.bitcast(I32), run.bitcast(I32)
                ch.step(V.tensor_copy(si, slot))
                ch.wait()
                ch.step(V.tensor_scalar(hi, si, 7, None, ALU.arith_shift_right))
                ch.step(V.tensor_scalar(slot.bitcast(I32), si, P - 1, None, ALU.bitwise_and))
                ch.wait()
                to = (recd[:, :, RW - 1], recs[:, :, SW - 1])[k]
                ch.step(V.scalar_tensor_tensor(out=to, in0=slot.bitcast(I32), scalar=float(TILES), in1=hi,
                                               op0=ALU.mult, op1=ALU.add))
                ch.wait()
                dve.sem_inc(slots_ready, 1)

            dve.wait_ge(s_ld["parts"], 16 * 7)

            def part(raw_ap, high, low):
                ch.step(V.tensor_copy(high, raw_ap))
                ch.wait()
                ch.step(V.tensor_tensor(low, raw_ap, high.bitcast(F32), ALU.subtract))

            part(st[:, 0, :], weh[:, :], wel[:, :])
            part(st[:, 1, :].rearrange("p (c o) -> p c o", c=KC), w2h[:, :, :], w2l[:, :, :])
            b2t = ts[0:64, 0, :]
            ch.step(V.memset(b2h[:, :].bitcast(F32), 0.0))
            ch.wait()
            ch.step(V.tensor_copy(b2h[:, :], b2w[:, :]))
            ch.wait()
            ch.step(V.tensor_tensor(b2t, b2w[:, :], b2h[:, :].bitcast(F32), ALU.subtract))
            ch.wait()
            ch.step(V.tensor_copy(b2h[32:33, :], b2t[32:33, :]))
            ch.wait()

            blk_regs = [dve.alloc_register(f"blk{j}") for j in range(BODY)]

            def load_blocks(k, c):
                dve.load(blk_regs, tbrow[0:1, k, bass.ds(c * BODY, BODY)])

            def make_hot(L, T, j, c):
                rw = WORDS[HALF[L]]
                par, s = j // U, j % U
                r = rec[:, par, s * rw:(s + 1) * rw].bitcast(F32)
                if s == 0:
                    dve.wait_ge(rec_in[par], (c + TURNS * L) * 16 + 16)
                if L == 0:
                    V.tensor_scalar(onehot[:, s, :], lane[:, :], r[:, 2:3], r[:, 3:4], ALU.is_equal, ALU.mult)\
                        .then_inc(hot[L], 1)
                else:
                    col = 2 if L == 2 else 1
                    V.tensor_scalar(onehot[:, s, :], lane[:, :], r[:, col:col + 1], None, ALU.is_equal)\
                        .then_inc(hot[L], 1)

            def add_tile(L, T, j, width, bank):
                b = dve.snap(blk_regs[j], min_val=0, max_val=USED - 1)
                dve.wait_ge(summed[L], T + 1)
                dve.wait_ge(done[L], T + BODY)
                a = acc_(b, width)
                V.tensor_tensor(a, a, bank[:, 0:width], ALU.add).then_inc(done[L], 1)

            def edge_adds(L, width):
                dve.wait_ge(acc_clear, L + 1)
                if L < 2:
                    dve.wait_ge(tb_back, 16 * (L + 1))
                LAG = 3
                with dve.Fori(0, TURNS) as c:
                    load_blocks(HALF[L], c)
                    for j in range(BODY + LAG):
                        if j < BODY:
                            make_hot(L, c * BODY + j, j, c)
                        if j >= LAG:
                            add_tile(L, c * BODY + j - LAG, j - LAG, width, ps[(j - LAG) % 4])

            def attr_low(c, jj):
                T, o = c * BODY + jj, jj % 2
                dve.wait_ge(e["atc"], T + 1)
                V.tensor_tensor(attrT[DE:P, o, :], ps[0][0:DE, 0:P], attrT[0:DE, o, :].bitcast(F32), ALU.subtract)\
                    .then_inc(e["atl"], 1)

            def hidden_low(c, jj):
                T, o = c * BODY + jj, jj % 2
                dve.wait_ge(e["relu"], T + 1)
                V.scalar_tensor_tensor(out=HTl[:, o, :, :].rearrange("p c n -> p (c n)"), in0=ps[1 + o][:, 0:D],
                                       scalar=0.0, in1=HTh[:, o, :, :].rearrange("p c n -> p (c n)").bitcast(F32),
                                       op0=ALU.max, op1=ALU.subtract).then_inc(e["htl"], 1)

            def gate_sum(c, jj):
                T, o = c * BODY + jj, jj % 2
                dve.wait_ge(e["gp"], T + 3)
                dve.wait_ge(e["sig"], T + 1)
                V.tensor_tensor(gs[:, o, :], ps[3 + o][:, 0:D], G[:, jj % U, D:2 * D], ALU.add).then_inc(e["gs"], 1)

            def message(c, jj):
                T, o = c * BODY + jj, jj % 2
                dve.wait_ge(e["sig"], T + 3)
                dve.wait_ge(e["core"], T + 3)
                V.tensor_tensor(msg[:, o, :], ps[5 + o][:, 0:D], sg[:, o, :], ALU.mult).then_inc(e["msg"], 1)

            def edge2_turn(c, first=False, last=False):
                if first:
                    load_blocks(0, c)
                for j in range(BODY):
                    if j == 2 and not first:
                        load_blocks(0, c)
                    make_hot(2, c * BODY + j, j, c)
                    if not (last and j == BODY - 1):
                        attr_low(c, j + 1)
                    hidden_low(c, j)
                    gate_sum(c, j)
                    if not first or j >= 1:
                        message(c, j - 1)
                    if not first or j >= 2:
                        add_tile(2, c * BODY + (j - 2), (j - 2) % BODY, D, ps[7])

            def edge2():
                dve.wait_ge(acc_clear, 3)
                attr_low(0, 0)
                edge2_turn(0, first=True)
                with dve.Fori(1, TURNS - 1) as c:
                    edge2_turn(c)
                edge2_turn(TURNS - 1, last=True)
                message(TURNS - 1, BODY - 1)
                for j in (BODY - 2, BODY - 1):
                    add_tile(2, (TURNS - 1) * BODY + j, j, D, ps[7])

            def finish_stats(L, which):
                ch.wait()
                s = stats[:, :, :]
                ch.step(V.tensor_tensor(lt[:, 0, :], s[:, :, 1], s[:, :, 4], ALU.add))
                ch.step(V.tensor_tensor(lt[:, 1, :], s[:, :, 1], s[:, :, 4], ALU.subtract))
                ch.step(V.tensor_tensor(rstd[:, :], s[:, :, 2], s[:, :, 5], ALU.add))
                ch.wait()
                ch.step(V.tensor_scalar(mean[:, :], lt[:, 0, :], 0.5, None, ALU.mult))
                ch.step(V.tensor_tensor(lt[:, 1, :], lt[:, 1, :], lt[:, 1, :], ALU.mult))
                ch.step(V.tensor_scalar(rstd[:, :], rstd[:, :], 1.0 / D, None, ALU.mult))
                ch.wait()
                ch.step(V.scalar_tensor_tensor(out=lt[:, 0, :], in0=lt[:, 1, :], scalar=0.25, in1=rstd[:, :],
                                               op0=ALU.mult, op1=ALU.add))
                ch.wait()
                dve.sem_inc(n[L]["var"], 1)
                dve.wait_ge(n[L]["std"], which + 1)
                ch.step(V.reciprocal(rstd[:, :], lt[:, 1, :]))
                ch.wait()

            def stat(b, of):
                V_out = stats[:, bass.ds(b, 1), :].rearrange("p a w -> p (a w)")
                ch.step(V.bn_stats(V_out, of))

            def normed(dst_ap, of, b):
                return V.tensor_scalar(dst_ap, of, mean[:, bass.ds(b, 1)], rstd[:, bass.ds(b, 1)],
                                       ALU.subtract, ALU.mult)

            def residual(L, relu):
                with dve.Fori(0, NB) as b:
                    ch.enter(b, 2)
                    if relu:
                        ch.step(V.scalar_tensor_tensor(out=X_(b), in0=acc_(b), scalar=0.0, in1=X_(b),
                                                       op0=ALU.max, op1=ALU.add))
                    else:
                        ch.step(V.tensor_tensor(X_(b), acc_(b), X_(b), ALU.add))
                    ch.wait()
                    stat(b, X_(b))
                    ch.leave(NB)
                ch.wait()

            def normalise_and_bias(L, width, bias):
                S = n[L]
                with dve.Fori(0, NB // 2) as c:
                    for par in range(2):
                        T = c * 2 + par
                        dve.wait_ge(S["xsc"], T + 1)
                        dve.wait_ge(S["tp"], T + 1)
                        normed(xs[:, par, :], X_(T), T).then_inc(S["xs"], 1)
                    for par in range(2):
                        T = c * 2 + par
                        dve.wait_ge(S["mm"], T + 3)
                        dve.wait_ge(S[f"sto{par}"], c * 16 + 16)
                        V.tensor_tensor(st[:, par, 0:width], ps[par][:, 0:width], bias, ALU.add).then_inc(S["st"], 1)

            edge_adds(0, D)
            dve.wait_ge(done[0], TILES + BODY)
            dve.wait_ge(s_ld["x"], 32)
            dve.wait_ge(s_ld["late"], 16 * LATE)
            residual(0, True)
            finish_stats(0, 0)
            dve.sem_inc(n[0]["accok"], 1)
            normalise_and_bias(0, D, rows["b_l1"][:, :])

            edge_adds(1, AW)
            dve.wait_ge(done[1], TILES + BODY)
            dve.wait_ge(n[0]["xsc"], NB + 2)
            residual(1, False)
            ch.step(V.tensor_scalar(rdeg[:, :], acc[:, :, D], 1.0, None, ALU.max))
            ch.wait()
            ch.step(V.reciprocal(rdeg[:, :], rdeg[:, :]))
            finish_stats(1, 0)
            dve.sem_inc(n[1]["accok"], 1)
            normalise_and_bias(1, 2 * D, bpg[:, :])

            edge2()
            dve.wait_ge(done[2], TILES + BODY)
            dve.wait_ge(n[1]["xsc"], NB + 2)
            with dve.Fori(0, NB) as b:
                ch.enter(b, 2)
                ch.step(V.tensor_tensor(acc_(b), acc_(b), X_(b), ALU.add))
                ch.wait()
                stat(b, acc_(b))
                ch.leave(NB)
            finish_stats(2, 0)
            with dve.Fori(0, NB) as b:
                ch.enter(b, 5)
                ch.step(normed(acc_(b), acc_(b), b))
                ch.wait()
                ch.step(V.tensor_tensor(acc_(b), acc_(b), rows["gamma"][:, :], ALU.mult))
                ch.wait()
                ch.step(V.tensor_tensor(acc_(b), acc_(b), rows["beta"][:, :], ALU.add))
                ch.wait()
                ch.step(V.tensor_tensor(acc_(b), acc_(b), X_(b), ALU.add))
                ch.wait()
                stat(b, acc_(b))
                ch.leave(NB)
            finish_stats(2, 1)
            with dve.Fori(0, NB // 2) as c:
                for par in range(2):
                    T = c * 2 + par
                    dve.wait_ge(n[2]["xsc"], T + 1)
                    dve.wait_ge(n[2][f"sto{par}"], c * 16 + 16)
                    normed(xs[:, par, :], acc_(T), T).then_inc(n[2]["xs"], 1)
            dve.wait_ge(n[2]["xs"], NB)
            dve.sem_inc(n[2]["accok"], 1)

            for L, bias, g, be in ((3, "b_a", "g_a", "be_a"), (4, "b_b", "g_b", "be_b")):
                S = n[L]
                edge_adds(L, D)
                dve.wait_ge(done[L], TILES + BODY)
                dve.wait_ge(n[L - 1]["xsc"], NB + 2)
                with dve.Fori(0, NB // 2) as c:
                    ch.enter(c, 2)
                    for par in range(2):
                        T = c * 2 + par
                        dve.wait_ge(S["tp"], T + 1)
                        V.scalar_tensor_tensor(out=xs[:, par, :], in0=acc_(T), scalar=rdeg[:, bass.ds(T, 1)],
                                               in1=X_(T), op0=ALU.mult, op1=ALU.add).then_inc(S["xs"], 1)
                    for par in range(2):
                        T = c * 2 + par
                        dve.wait_ge(S["mm"], T + 3)
                        V.tensor_tensor(acc_(T), ps[par][:, 0:D], rows[bias][:, :], ALU.add).then_inc(S["st"], 1)
                        dve.wait_ge(S["st"], T + 3)
                        stat(T, acc_(T))
                    ch.leave(NB // 2)
                finish_stats(L, 0)
                with dve.Fori(0, NB // 2) as c:
                    ch.enter(c, 4 if L == 3 else 8)
                    for par in range(2):
                        T = c * 2 + par
                        t = ts[:, par, :]
                        dve.wait_ge(S["ys"], T + 1)
                        ch.step(normed(t, acc_(T), T))
                        ch.wait()
                        ch.step(V.tensor_tensor(t, t, rows[g][:, :], ALU.mult))
                        ch.wait()
                        V.tensor_tensor(t, t, rows[be][:, :], ALU.add).then_inc(S["ts"], 1)
                    for par in range(2):
                        T = c * 2 + par
                        dve.wait_ge(S["sg"], T + 1)
                        if L == 3:
                            dve.wait_ge(S["xsc"], T + 1)
                            dve.wait_ge(S[f"sto{par}"], c * 16 + 16)
                            V.tensor_tensor(st[:, par, 0:D], ts[:, par, :], sg[:, par, :], ALU.mult).then_inc(S["ys"], 1)
                        else:
                            V.tensor_tensor(X_(T), ts[:, par, :], sg[:, par, :], ALU.mult).then_inc(S["ys"], 1)
                            dve.wait_ge(S["ys"], T + 3)
                            dve.wait_ge(x3_in[par], c * 16 + 16)
                            ch.step(V.tensor_tensor(X_(T), X_(T), xs[:, par, :], ALU.add))
                            ch.wait()
                            stat(T, X_(T))
                            ch.wait()
                            dve.sem_inc(x3_used, 1)
                    ch.leave(NB // 2)
                if L == 3:
                    dve.wait_ge(S["ys"], NB + 2)
                    dve.sem_inc(S["accok"], 1)
            finish_stats(4, 1)
            with dve.Fori(0, NB // 2) as c:
                for par in range(2):
                    T = c * 2 + par
                    dve.wait_ge(n[4][f"sto{par}"], c * 16 + 16)
                    normed(st[:, par, 0:D], X_(T), T).then_inc(out_ready, 1)

        @block.scalar
        def _(act):
            A = nc.scalar

            def into_X(sem_, value, T, of):
                act.wait_ge(sem_, value)
                act.sem_inc(act_ok, 1)
                return A.activation(X_(T), of, ACT.Copy)

            act.wait_ge(s_ld["x"], 32)
            act.wait_ge(raw_used, 1)
            trows = t_rel.rearrange("(m r) d -> m (r d)", r=R)
            with act.Fori(0, NB // 2) as c:
                for par in range(2):
                    T = c * 2 + par
                    act.wait_ge(q["xt"], T + 1)
                    act.sem_inc(act_ok, 1)
                    A.activation(xs[:, par, :], X_(T), ACT.Copy).then_inc(q["xs"], 1)
                    act.wait_ge(q["xt"], T + 3)
                    A.activation(xT[:, par, :, :], ps[4 + par][:, 0:D].rearrange("p (c n) -> p c n", c=KC), ACT.Copy)\
                        .then_inc(q["xtc"], 1)
                    act.wait_ge(q["pg"], T + 1)
                    A.activation(gate[:, par, :], ps[6][:, 0:R], ACT.Sigmoid).then_inc(q["gate"], 1)
                    act.wait_ge(q["gate"], T + 2)
                    for g in range(R // 2):
                        h = g // 4
                        act.wait_ge(q["pr"], T * (R // 2) + (g + 1))
                        if g % 4 == 0:
                            act.wait_ge(q[f"st{h}"], T * 16 + 16)
                        for r in range(2):
                            A.activation(stage[:, h, ((g % 4) * 2 + r) * D:((g % 4) * 2 + r + 1) * D],
                                         ps[g % 4][:, r * D:(r + 1) * D], ACT.Copy,
                                         scale=gate[:, par, 2 * g + r:2 * g + r + 1]).then_inc(q["ev"], 1)
                        if g % 4 == 3:
                            act.wait_ge(q["ev"], T * R + (8 * (h + 1) + 8))
                            act.dma_start(trows[bass.ds(T * P, P), h * 8 * D:(h + 1) * 8 * D], stage[:, h, :])\
                               .then_inc(q[f"st{h}"], 16)

            def std(L, which):
                act.wait_ge(n[L]["var"], which + 1)
                A.activation(lt[:, 1, :], lt[:, 0, :], ACT.Sqrt, bias=epsc[:, 0:1]).then_inc(n[L]["std"], 1)

            def transposed(L, T, par):
                S = n[L]
                act.wait_ge(S["tp"], T + 3)
                act.wait_ge(S["mm"], T + 1)
                A.activation(xT[:, par, :, :], ps[6 + par][:, 0:D].rearrange("p (c n) -> p c n", c=KC), ACT.Copy)\
                    .then_inc(S["tpc"], 1)

            def node_plain(L):
                std(L, 0)
                with act.Fori(0, NB // 2) as c:
                    for par in range(2):
                        T = c * 2 + par
                        into_X(n[L]["xs"], T + 1, T, xs[:, par, :]).then_inc(n[L]["xsc"], 1)
                        transposed(L, T, par)

            node_plain(0)
            node_plain(1)

            def attr_high(T, jj):
                act.wait_ge(e["at"], T + 1)
                act.wait_ge(e["gp"], T + 1)
                A.activation(attrT[0:DE, jj % 2, :], ps[0][0:DE, 0:P], ACT.Copy).then_inc(e["atc"], 1)

            def act_step(T, j, last=False):
                if not last:
                    attr_high(T + 1, j + 1)
                act.wait_ge(e["ht"], T + 1)
                act.wait_ge(e["core"], T + 1)
                A.activation(HTh[:, j % 2, :, :], ps[1 + j % 2][:, 0:D].rearrange("p (c n) -> p c n", c=KC), ACT.Relu)\
                    .then_inc(e["relu"], 1)
                act.wait_ge(e["gs"], T + 3)
                act.wait_ge(e["msg"], T + 1)
                A.activation(sg[:, j % 2, :], gs[:, j % 2, :], ACT.Sigmoid).then_inc(e["sig"], 1)

            attr_high(0, 0)
            with act.Fori(0, TURNS - 1) as c:
                for j in range(BODY):
                    act_step(c * BODY + j, j)
            for j in range(BODY):
                act_step((TURNS - 1) * BODY + j, j, j == BODY - 1)

            std(2, 0)
            std(2, 1)
            with act.Fori(0, NB // 2) as c:
                for par in range(2):
                    T = c * 2 + par
                    into_X(n[2]["xs"], T + 1, T, xs[:, par, :]).then_inc(n[2]["xsc"], 1)

            for L in (3, 4):
                S = n[L]
                with act.Fori(0, NB // 2) as c:
                    for par in range(2):
                        transposed(L, c * 2 + par, par)
                std(L, 0)
                with act.Fori(0, NB // 2) as c:
                    for par in range(2):
                        T = c * 2 + par
                        act.wait_ge(S["ts"], T + 1)
                        act.wait_ge(S["ys"], T + 1)
                        A.activation(sg[:, par, :], ts[:, par, :], ACT.Sigmoid).then_inc(S["sg"], 1)
                    if L == 3:
                        for par in range(2):
                            T = c * 2 + par
                            into_X(S["ys"], T + 3, T, st[:, par, 0:D]).then_inc(S["xsc"], 1)
            std(4, 1)

        @block.tensor
        def _(pe):
            T_ = nc.tensor

            pe.wait_ge(consts, 12)
            pe.wait_ge(counted, 2)
            for k in range(2):
                for h, m in enumerate((tri, ones)):
                    last = T_.matmul(ps[7][:, (2 * k + h) * P:(2 * k + h) * P + USED], m[0:EPP, :],
                                     cnt[0:EPP, k, 0:USED], start=True, stop=True)
            last.then_inc(based, 1)

            pe.wait_ge(s_ld["wgate"], 16)
            pe.wait_ge(s_ld["wrel"], 32)
            with pe.Fori(0, NB // 2) as c:
                for par in range(2):
                    T = c * 2 + par
                    pe.wait_ge(q["xs"], T + 1)
                    pe.wait_ge(q["xtc"], T + 1)
                    for k in range(KC):
                        last = T_.transpose(ps[4 + par][:, k * P:(k + 1) * P], xs[:, par, k * P:(k + 1) * P], ident[:, :])
                    last.then_inc(q["xt"], 1)
                    pe.wait_ge(q["xtc"], T + 3)
                    pe.wait_ge(q["gate"], T + 1)
                    for k in range(KC):
                        last = T_.matmul(ps[6][:, 0:R], xT[:, par, k, :], wgate[:, k, :], start=k == 0, stop=k == KC - 1)
                    last.then_inc(q["pg"], 1)
                    for g in range(R // 2):
                        pe.wait_ge(q["ev"], T * R + (2 * g + 2))
                        for k in range(KC):
                            last = T_.matmul(ps[g % 4][:, :], xT[:, par, k, :], wrel[:, k, g * 2 * D:(g + 1) * 2 * D],
                                             start=k == 0, stop=k == KC - 1)
                        last.then_inc(q["pr"], 1)

            def rows_in(semaphores, L, c, jj):
                pe.wait_ge(semaphores[jj % U], (c * 2 + (jj // U + 1 + (2 * TURNS * L if semaphores is gathered else 0))) * 16)

            def edge_sums(L, width):
                with pe.Fori(0, TURNS) as c:
                    for j in range(BODY):
                        pe.wait_ge(hot[L], c * BODY + j + 1)
                        rows_in(gathered, L, c, j)
                        pe.wait_ge(done[L], c * BODY + j + (1 + BODY - 4))
                        T_.matmul(ps[j % 4][:, 0:width], onehot[:, j % U, :], G[:, j % U, 0:width],
                                  start=True, stop=True).then_inc(summed[L], 1)

            def transposes(L, T, par):
                S = n[L]
                pe.wait_ge(S["xs"], T + 1)
                pe.wait_ge(S["tpc"], T + 1)
                for k in range(KC):
                    last = T_.transpose(ps[6 + par][:, k * P:(k + 1) * P], xs[:, par, k * P:(k + 1) * P], ident[:, :])
                last.then_inc(S["tp"], 1)

            def products(L, weights, width):
                S = n[L]
                with pe.Fori(0, NB // 2) as c:
                    for par in range(2):
                        transposes(L, c * 2 + par, par)
                    for par in range(2):
                        T = c * 2 + par
                        pe.wait_ge(S["tpc"], T + 3)
                        pe.wait_ge(S["st"], T + 1)
                        for k in range(KC):
                            last = T_.matmul(ps[par][:, 0:width], xT[:, par, k, :], weights[:, k, :],
                                             start=k == 0, stop=k == KC - 1)
                        last.then_inc(S["mm"], 1)

            edge_sums(0, D)
            pe.wait_ge(s_ld["late"], 16 * LATE)
            products(0, wl1, D)
            pe.wait_ge(ones_in, 1)
            edge_sums(1, AW)
            products(1, wpg, 2 * D)

            def A(c, jj):
                rows_in(attr_in, 2, c, jj)
                pe.wait_ge(e["atl"], c * BODY + (jj + 1))
                pe.sem_inc(pe_ok, 1)
                T_.transpose(ps[0][0:DE, 0:P], attr[:, jj % U, :], ident[:, :]).then_inc(e["at"], 1)

            def B(c, jj):
                T, s = c * BODY + jj, jj % U
                rows_in(gathered, 2, c, jj)
                pe.wait_ge(e["atl"], T + 2)
                pe.wait_ge(e["htl"], T + 1)
                for k in range(KC):
                    o = ps[1 + jj % 2][:, k * P:(k + 1) * P]
                    T_.matmul(o, G[:, s, k * P:(k + 1) * P], ident[:, :], is_transpose=True, start=True, stop=False)
                    T_.matmul(o, weh[:, k * P:(k + 1) * P], attrT[:, jj % 2, :], start=False, stop=False)
                    last = T_.matmul(o, wel[:, k * P:(k + 1) * P], attrT[:, jj % 2, :], start=False, stop=True)
                last.then_inc(e["ht"], 1)
                pe.wait_ge(e["gs"], T + 1)
                o = ps[3 + jj % 2][:, 0:D]
                T_.matmul(o, attrT[:, jj % 2, :], weh[:, D:2 * D], start=True, stop=False)
                T_.matmul(o, attrT[:, jj % 2, :], wel[:, D:2 * D], start=False, stop=True).then_inc(e["gp"], 1)

            def C(c, jj):
                T = c * BODY + jj
                pe.wait_ge(e["htl"], T + 3)
                pe.wait_ge(e["msg"], T + 1)
                o = ps[5 + jj % 2][:, 0:D]
                for k in range(KC):
                    for n_, (a, b) in enumerate(((HTh, w2h), (HTh, w2l), (HTl, w2h))):
                        T_.matmul(o, a[:, jj % 2, k, :], b[:, k, :], start=k == 0 and n_ == 0, stop=False)
                T_.matmul(o, ones_r[:, :], b2h[:, :], start=False, stop=True).then_inc(e["core"], 1)

            def D_(c, jj):
                T = c * BODY + jj
                pe.wait_ge(hot[2], T + 1)
                pe.wait_ge(e["msg"], T + 3)
                pe.wait_ge(done[2], T + BODY)
                T_.matmul(ps[7][:, 0:D], onehot[:, jj % U, :], msg[:, jj % 2, :], start=True, stop=True)\
                    .then_inc(summed[2], 1)

            def pe_turn(c, first=False, last=False):
                for j in range(BODY):
                    if not (last and j == BODY - 1):
                        A(c, j + 1)
                    B(c, j)
                    if not first or j >= 1:
                        C(c, j - 1)
                    if not first or j >= 2:
                        D_(c, j - 2)

            A(0, 0)
            pe_turn(0, first=True)
            with pe.Fori(1, TURNS - 1) as c:
                pe_turn(c)
            pe_turn(TURNS - 1, last=True)
            C(TURNS - 1, BODY - 1)
            D_(TURNS - 1, BODY - 2)
            D_(TURNS - 1, BODY - 1)

            for L in (3, 4):
                edge_sums(L, D)
                products(L, wab[:, L - 3], D)


_OUT = ((N, D), "float32")


def kernel(x, src, dst, edge_attr_64, edge_type_16, edge_weight1, L0_gnn_weight, L0_gnn_gate_weight,
           L1_gnn_W, L1_gnn_b, L2_gnn_W1, L2_gnn_b1, L2_gnn_W2, L2_gnn_b2, L2_gnn_Wg, L2_gnn_bg,
           L2_gnn_gamma, L2_gnn_beta, L3_gnn_W0, L3_gnn_b0, L3_gnn_g0, L3_gnn_beta0, L3_gnn_W1,
           L3_gnn_b1, L3_gnn_g1, L3_gnn_beta1):
    import numpy as np
    import concourse.bacc as bacc
    from concourse.bass_utils import run_bass_kernel_spmd

    given = [
        ("x", x), ("src", src), ("dst", dst), ("edge_attr", edge_attr_64), ("edge_type", edge_type_16),
        ("edge_weight", edge_weight1), ("w_rel", L0_gnn_weight),
        ("w_gate", np.asarray(L0_gnn_gate_weight)[:, :, 0].T), ("w_l1", np.asarray(L1_gnn_W).T), ("b_l1", L1_gnn_b),
        ("w1", L2_gnn_W1), ("b1", L2_gnn_b1), ("w2", L2_gnn_W2), ("b2", L2_gnn_b2), ("wg", L2_gnn_Wg), ("bg", L2_gnn_bg),
        ("gamma", L2_gnn_gamma), ("beta", L2_gnn_beta),
        ("w_a", np.asarray(L3_gnn_W0).T), ("b_a", L3_gnn_b0), ("g_a", L3_gnn_g0), ("be_a", L3_gnn_beta0),
        ("w_b", np.asarray(L3_gnn_W1).T), ("b_b", L3_gnn_b1), ("g_b", L3_gnn_g1), ("be_b", L3_gnn_beta1),
    ]
    nc = bacc.Bacc("TRN2", target_bir_lowering=False, num_devices=1)
    arrays, args = {}, {}
    for name, a in given:
        a = np.ascontiguousarray(a)
        arrays[f"in_{name}"] = a
        args[name] = nc.dram_tensor(f"in_{name}", a.shape, mybir.dt.from_np(a.dtype), kind="ExternalInput").ap()
    args["out"] = nc.dram_tensor("out_0", _OUT[0], mybir.dt.from_np(np.dtype(_OUT[1])), kind="ExternalOutput").ap()
    program(nc, **args)
    r = run_bass_kernel_spmd(nc, [arrays], core_ids=[0])
    return r.results[0]["out_0"]
```

```python
from contextlib import ExitStack

import concourse.bass as bass
from concourse import mybir

ALU = mybir.AluOpType
ACT = mybir.ActivationFunctionType
F32 = mybir.dt.float32
I32 = mybir.dt.int32
R32 = mybir.dt.float32r

P = 128
N, D = 6250, 256
E, DE, R = 100000, 64, 16
KC = D // P
NB = 50
FULL = N // P
TAIL = N - FULL * P
EPP = 125
EPT = E // EPP
USED = FULL + 1
TILES = 832
SLOTS = TILES * P
U = 8
BODY = 2 * U
TURNS = TILES // BODY
SC = 16
SCHUNKS = EPT // SC
RW = 6
SW = 3
LATE = 16
AW = D + 1
EPS = 1e-5
TB = 7
assert TILES * P >= E + USED * (P - 1) and TILES % BODY == 0 and EPT % (2 * SC) == 0


class Chain:

    def __init__(self, eng, sem):
        self.eng, self.sem, self.base, self.n = eng, sem, 0, 0

    def step(self, ins):
        ins.then_inc(self.sem, 1)
        self.n += 1

    def wait(self):
        self.eng.wait_ge(self.sem, self.base + self.n)

    def enter(self, i, per):
        self.outer, self.per = self.base + self.n, per
        self.base, self.n = self.outer + i * per, 0

    def leave(self, turns):
        assert self.n == self.per, (self.n, self.per)
        self.base, self.n = self.outer + turns * self.per, 0


def program(nc, x, src, dst, edge_attr, edge_type, edge_weight, w_rel, w_gate, w_l1, b_l1,
            w1, b1, w2, b2, wg, bg, gamma, beta, w_a, b_a, g_a, be_a, w_b, b_b, g_b, be_b, out):
    ctx = ExitStack()
    with ctx:
        def sb(name, shape, dt=F32):
            return ctx.enter_context(nc.sbuf_tensor(name, shape, dt))

        def sem(name):
            return ctx.enter_context(nc.semaphore(name))

        t_rel = nc.dram_tensor("t_rel", (NB * P * R, D), F32).ap()
        t_h = nc.dram_tensor("t_h", (NB * P, D), F32).ap()
        t_pg = nc.dram_tensor("t_pg", (NB * P, 2 * D), F32).ap()
        t_x3 = nc.dram_tensor("t_x3", (NB * P, D), F32).ap()
        t_y1 = nc.dram_tensor("t_y1", (NB * P, D), F32).ap()
        r_dst = nc.dram_tensor("r_dst", (SLOTS, RW), I32).ap()
        r_src = nc.dram_tensor("r_src", (SLOTS, SW), I32).ap()
        d_tb = nc.dram_tensor("d_tb", (3, TB * P), I32).ap()
        d_tf = nc.dram_tensor("d_tf", (1, TB * P), F32).ap()

        X = sb("X", [P, NB, D])
        acc = sb("acc", [P, NB, AW])
        accf = acc[:, :, :].rearrange("p b w -> p (b w)")
        wrel = accf[:, 0:KC * R * D].rearrange("p (c n) -> p c n", c=KC)
        o = KC * R * D
        blk = {k: accf[0:EPP, o + n * EPT:o + (n + 1) * EPT] for n, k in enumerate(("dst", "src"))}
        ind, run, slot = (accf[0:EPP, o + n * EPT:o + (n + 1) * EPT] for n in (2, 3, 4))
        arena = sb("arena", [P, 4096])
        stage = arena[:, :].rearrange("p (s n) -> p s n", s=2)
        raw = arena[0:EPP, 0:5 * EPT].rearrange("p (k t) -> p k t", k=5)
        G = arena[:, :].rearrange("p (s n) -> p s n", s=U)
        early = sb("early", [P, EPT * RW])
        recd = early[0:EPP, :].bitcast(I32).rearrange("p (t w) -> p t w", w=RW)
        recs = sb("recs", [EPP, EPT, SW], I32)
        scat = sb("scat", [EPP, 2, SC * RW], I32)
        tmpl = sb("tmpl", [P, U * RW], I32)
        tmpls = sb("tmpls", [P, U * SW], I32)
        rec = sb("rec", [P, 2, U * RW], I32)
        lane = sb("lane", [P, P])
        ident = sb("ident", [P, P])
        ones = sb("ones", [P, P])
        tri = sb("tri", [P, P])
        tcol = sb("tcol", [P, TB])
        zero = sb("zero", [P, 1])
        epsc = sb("epsc", [P, 1])
        cnt = sb("cnt", [P, 2, P])
        blks = sb("blks", [P, 8, 64])
        blki = sb("blki", [P, 64], I32)
        tbf = sb("tbf", [P, 4, TB])
        tbi = sb("tbi", [P, 3, TB], I32)
        tbrow = sb("tbrow", [1, 3, TILES], I32)
        node0 = sb("node0", [P, TILES])
        local = sb("local", [P, 2, U])
        flag = sb("flag", [P, 2])
        flagi = sb("flagi", [P, 1], I32)
        tj = sb("tj", [P, 64])
        wgate = sb("wgate", [P, KC, R])
        wl1 = sb("wl1", [P, KC, D])
        wpg = sb("wpg", [P, KC, 2 * D])
        weh, wel = sb("weh", [P, 2 * D], R32), sb("wel", [P, 2 * D], R32)
        w2h, w2l = sb("w2h", [P, KC, D], R32), sb("w2l", [P, KC, D], R32)
        wab = sb("wab", [P, 2, KC, D])
        bpg = sb("bpg", [P, 2 * D])
        b2w = sb("b2w", [64, D])
        b2h = sb("b2h", [64, D], R32)
        ones_r = sb("ones_r", [64, P], R32)
        rows, row8, o = {}, sb("row8", [P, D]), 2 * U * P + 2 * D
        for name in ("b_l1", "gamma", "beta", "b_a", "g_a", "be_a", "b_b", "g_b", "be_b"):
            k = len(rows)
            rows[name] = row8[:, :] if k == 8 else early[:, o + k * D:o + (k + 1) * D]
        gate = sb("gate", [P, 2, R])
        xs = sb("xs", [P, 2, D])
        xT = sb("xT", [P, 2, KC, P])
        ts = sb("ts", [P, 2, D])
        st = sb("st", [P, 2, 2 * D])
        stats = sb("stats", [P, NB, 6])
        mean = sb("mean", [P, NB])
        rstd = sb("rstd", [P, NB])
        lt = sb("lt", [P, 2, NB])
        rdeg = sb("rdeg", [P, NB])
        onehot = early[:, 0:U * P].rearrange("p (s n) -> p s n", s=U)
        attr = early[:, U * P:U * P + BODY * DE].rearrange("p (s n) -> p s n", s=BODY)
        sg = early[:, 2 * U * P:2 * U * P + 2 * D].rearrange("p (s n) -> p s n", s=2)
        attrT = sb("attrT", [P, 2, P], R32)
        HTh, HTl = sb("HTh", [P, 2, KC, P], R32), sb("HTl", [P, 2, KC, P], R32)
        gs, msg = xs, ts

        ps = [ctx.enter_context(nc.psum_tensor(f"ps{i}", [P, 512], F32)) for i in range(8)]

        s_ld = {k: sem("ld_" + k) for k in ("edges", "x", "wrel", "wgate", "parts", "late")}
        xpad = sem("xpad")
        consts = sem("consts")
        tmpl_ready, prefilled = sem("tmpl_ready"), sem("prefilled")
        v_sem, a_sem = sem("v_chain"), sem("a_chain")
        raw_used = sem("raw_used")
        counted, based = sem("counted"), sem("based")
        slots_ready = [sem(f"slots_ready{k}") for k in range(2)]
        scratch_free = sem("scratch_free")
        v_branch = sem("v_branch")
        listed = sem("listed")
        tb_ready, tb_stored, tb_back = sem("tb_ready"), sem("tb_stored"), sem("tb_back")
        scat_in = [[sem(f"scat_in{k}{i}") for i in range(2)] for k in range(2)]
        scattered = [[sem(f"scattered{k}{i}") for i in range(2)] for k in range(2)]
        went_on = sem("went_on")
        q = {k: sem("q_" + k) for k in ("xs", "xt", "xtc", "pg", "pr", "gate", "ev", "st0", "st1")}
        acc_clear = sem("acc_clear")
        b2_clear = sem("b2_clear")
        located = sem("located")
        ones_in = sem("ones_in")
        rec_in = [sem(f"rec_in{i}") for i in range(2)]
        gathered = [sem(f"gathered{i}") for i in range(U)]
        attr_in = [sem(f"attr_in{i}") for i in range(2)]
        hot = [sem(f"hot{L}") for L in range(5)]
        summed = [sem(f"summed{L}") for L in range(5)]
        done = [sem(f"done{L}") for L in range(5)]
        e = {k: sem("e_" + k) for k in ("at", "atc", "atl", "ht", "relu", "htl", "gp", "gs", "sig", "core", "msg")}
        node_sems = ["var", "std", "xs", "xsc", "sto0", "sto1", "accok"]
        product_sems = ["tp", "tpc", "mm", "st"]
        silu_sems = ["ts", "sg", "ys"]
        n = [{k: sem(f"n{L}_{k}") for k in node_sems + product_sems * (L != 2) + silu_sems * (L > 2)} for L in range(5)]
        x3_in = [sem(f"x3_in{i}") for i in range(2)]
        x3_used, out_ready = sem("x3_used"), sem("out_ready")

        block = ctx.enter_context(nc.Block())

        HALF = {0: 0, 1: 1, 2: 0, 3: 1, 4: 1}
        VIEW = [r_dst.rearrange("(p t) w -> p (t w)", p=P), r_src.rearrange("(p t) w -> p (t w)", p=P)]
        WORDS = [RW, SW]
        PER = [16 * U if HALF[L] == 0 else 16 for L in range(5)]
        BEFORE = [TURNS * sum(PER[:L]) for L in range(5)]

        def X_(b):
            return X[:, bass.ds(b, 1), :].rearrange("p a w -> p (a w)")

        def acc_(b, w=D):
            return acc[:, bass.ds(b, 1), 0:w].rearrange("p a w -> p (a w)")

        @block.sync
        def _(sp):
            def load(name, dst_ap, src_ap):
                sp.dma_start(dst_ap, src_ap).then_inc(s_ld[name], 16)

            for L in range(5):
                sp.sem_inc(done[L], BODY)
                for k, v in (("xsc", 2), ("tp", 2), ("tpc", 2), ("mm", 2), ("st", 2), ("ys", 2), ("sto0", 16), ("sto1", 16)):
                    if k in n[L]:
                        sp.sem_inc(n[L][k], v)
            for k, v in (("xt", 2), ("xtc", 2), ("gate", 1), ("ev", 8), ("st0", 16), ("st1", 16)):
                sp.sem_inc(q[k], v)
            for k, v in (("atl", 1), ("gp", 2), ("core", 2), ("msg", 2), ("htl", 2), ("gs", 2), ("sig", 2)):
                sp.sem_inc(e[k], v)
            sp.sem_inc(x3_used, 2)

            for k, a in enumerate((src, dst, edge_type)):
                load("edges", raw[:, k, :].bitcast(I32), a.rearrange("(p t) -> p t", p=EPP))
            load("edges", raw[0:EPP - 1, 4, :].bitcast(I32), dst[1:E - EPT + 1].rearrange("(p t) -> p t", p=EPP - 1))
            load("edges", raw[EPP - 1:EPP, 4, 0:EPT - 1].bitcast(I32), dst[E - EPT + 1:E].unsqueeze(0))
            load("edges", raw[EPP - 1:EPP, 4, EPT - 1:EPT].bitcast(I32), dst[E - 1:E].unsqueeze(0))
            load("edges", raw[:, 3, :], edge_weight.rearrange("(p t) a -> p (t a)", p=EPP))
            load("x", X[:, 0:FULL, :], x[0:FULL * P, :].rearrange("(b p) f -> p b f", p=P))
            sp.wait_ge(xpad, 1)
            load("x", X[0:TAIL, FULL, :], x[FULL * P:N, :])
            load("wgate", wgate[:, :, :], w_gate.rearrange("(c p) r -> p c r", p=P))
            for c in range(KC):
                load("wrel", wrel[:, c, :].rearrange("p (r o) -> p r o", r=R),
                     w_rel[:, c * P:(c + 1) * P, :].rearrange("r p o -> p r o"))
            sp.wait_ge(tmpl_ready, 2)
            for view, t, w in ((VIEW[0], tmpl, RW), (VIEW[1], tmpls, SW)):
                for k in range(4):
                    n_rep = TILES // U // 4
                    sp.dma_start(view[:, k * n_rep * U * w:(k + 1) * n_rep * U * w].rearrange("p (a w) -> p a w", a=n_rep),
                                 t[:, :].unsqueeze(1).broadcast_to([P, n_rep, U * w])).then_inc(prefilled, 16)
            for h in range(2):
                for k, w in enumerate((w1, wg)):
                    load("parts", st[h * DE:(h + 1) * DE, 0, k * D:(k + 1) * D], w[D:D + DE, :])
            load("parts", st[:, 1, :].rearrange("p (c o) -> p c o", c=KC), w2.rearrange("(c p) o -> p c o", p=P))
            sp.wait_ge(b2_clear, 1)
            for r in (0, 32):
                load("parts", b2w[r:r + 1, :], b2.rearrange("(a d) -> a d", a=1))
            for a, b in ((wl1[:, :, :], w_l1), (wab[:, 0], w_a), (wab[:, 1], w_b),
                         (wpg[:, :, 0:D], w1[0:D, :]), (wpg[:, :, D:2 * D], wg[0:D, :])):
                load("late", a, b.rearrange("(c p) o -> p c o", p=P))
            load("late", bpg[:, 0:D], b1.partition_broadcast(P))
            load("late", bpg[:, D:2 * D], bg.partition_broadcast(P))

            def scatter_chunks(k):
                sp.wait_ge(slots_ready[k], 1)
                rw = WORDS[k]
                big = (recd, recs)[k].rearrange("p t w -> p (t w)")
                for par in range(2):
                    if k == 0:
                        sp.wait_ge(scattered[1][par], 16 * SC * (SCHUNKS // 2))
                    sp.dma_start(scat[:, par, 0:SC * rw], big[:, par * SC * rw:(par + 1) * SC * rw])\
                      .then_inc(scat_in[k][par], 16)
                with sp.Fori(1, SCHUNKS // 2) as c:
                    for par in range(2):
                        sp.wait_ge(scattered[k][par], c * (16 * SC))
                        sp.dma_start(scat[:, par, 0:SC * rw], big[:, bass.ds((c * 2 + par) * (SC * rw), SC * rw)])\
                          .then_inc(scat_in[k][par], 16)
                for par in range(2):
                    sp.wait_ge(scattered[k][par], 16 * SC * (SCHUNKS // 2))

            def tile_tables():
                sp.wait_ge(tb_ready, 1)
                for k in range(3):
                    sp.dma_start(d_tb[k, :].rearrange("(p j) -> p j", p=P), tbi[:, k, :]).then_inc(tb_stored, 16)
                sp.dma_start(d_tf[0, :].rearrange("(p j) -> p j", p=P), tbf[:, 3, :]).then_inc(tb_stored, 16)
                sp.wait_ge(tb_stored, 64)
                for k in range(3):
                    sp.dma_start(tbrow[:, k, :], d_tb[k:k + 1, 0:TILES]).then_inc(tb_back, 16)
                sp.dma_start(node0[:, :], d_tf[0, 0:TILES].partition_broadcast(P)).then_inc(tb_back, 16)

            first_regs = [sp.alloc_register(f"first{j}") for j in range(BODY)]

            def record_chunks(L, features=False):
                k = HALF[L]
                w = U * WORDS[k]
                with sp.Fori(0, TURNS) as c:
                    if k == 0:
                        sp.load(first_regs, tbrow[0:1, 2, bass.ds(c * BODY, BODY)])
                    for par in range(2):
                        sp.wait_ge(done[L], c * BODY + par * U + U)
                        if k == 1:
                            sp.dma_start(rec[:, par, 0:w], VIEW[k][:, bass.ds((c * 2 + par) * w, w)])\
                              .then_inc(rec_in[par], 16)
                            continue
                        firsts = [sp.snap(first_regs[par * U + s], min_val=0, max_val=SLOTS - P) for s in range(U)]
                        for s in range(U):
                            sp.dma_start(rec[:, par, s * RW:(s + 1) * RW], r_dst[bass.ds(firsts[s], P), :])\
                              .then_inc(rec_in[par], 16)
                        if features:
                            for s in range(U):
                                sp.dma_start(attr[:, par * U + s, :], edge_attr[bass.ds(firsts[s], P), :])\
                                  .then_inc(attr_in[par], 16)

            def store_blocks(L, table, buf, ready, credits):
                with sp.Fori(0, NB // 2) as c:
                    for par in range(2):
                        sp.wait_ge(ready, c * 2 + par + (1 + credits))
                        sp.dma_start(table[bass.ds((c * 2 + par) * P, P), :], buf[par])\
                          .then_inc(n[L][f"sto{par}"], 16)

            tile_tables()
            sp.wait_ge(tb_back, 64)
            in_order = sp.value_load(flagi[0:1, 0:1], min_val=0, max_val=1)
            sp.wait_ge(prefilled, 16 * 8)
            with sp.If(in_order == 1):
                sp.dma_start(r_dst[0:E, :].rearrange("(p t) w -> p (t w)", p=EPP), recd.rearrange("p t w -> p (t w)"))\
                  .then_inc(listed, 16)
                sp.wait_ge(listed, 16)
            scatter_chunks(1)
            with sp.If(in_order == 0):
                scatter_chunks(0)
            for name, a in (("b_l1", b_l1), ("gamma", gamma), ("beta", beta), ("b_a", b_a), ("g_a", g_a),
                            ("be_a", be_a), ("b_b", b_b), ("g_b", g_b), ("be_b", be_b)):
                load("late", rows[name][:, :], a.partition_broadcast(P))
            record_chunks(0)
            store_blocks(0, t_h, [st[:, par, 0:D] for par in range(2)], n[0]["st"], 2)
            record_chunks(1)
            store_blocks(1, t_pg, [st[:, par, :] for par in range(2)], n[1]["st"], 2)
            with sp.If(in_order == 1):
                record_chunks(2, features=True)
            with sp.Else():
                record_chunks(2)
            store_blocks(2, t_x3, [xs[:, par, :] for par in range(2)], n[2]["xs"], 0)
            record_chunks(3)
            store_blocks(3, t_y1, [st[:, par, 0:D] for par in range(2)], n[3]["ys"], 2)
            record_chunks(4)
            sp.wait_ge(n[4]["mm"], NB + 2)
            with sp.Fori(0, NB // 2) as c:
                for par in range(2):
                    sp.wait_ge(x3_used, c * 2 + par + 1)
                    sp.dma_start(xs[:, par, :], t_x3[bass.ds((c * 2 + par) * P, P), :]).then_inc(x3_in[par], 16)
            with sp.Fori(0, FULL // 2) as c:
                for par in range(2):
                    sp.wait_ge(out_ready, c * 2 + par + 1)
                    sp.dma_start(out[bass.ds((c * 2 + par) * P, P), :], st[:, par, 0:D]).then_inc(n[4][f"sto{par}"], 16)
            sp.wait_ge(out_ready, FULL + 1)
            sp.dma_start(out[FULL * P:N, :], st[0:TAIL, 0, 0:D]).then_inc(n[4]["sto0"], 16)
            sp.wait_ge(n[4]["sto0"], 16 * (FULL // 2 + 1) + 16)
            sp.wait_ge(n[4]["sto1"], 16 * (FULL // 2) + 16)

        @block.gpsimd
        def _(pool):
            pool.memset(X[:, FULL:NB, :], 0.0).then_inc(xpad, 1)
            pool.memset(ones[:, :], 1.0).then_inc(consts, 1)
            pool.memset(ident[:, :], 0.0).then_inc(consts, 1)
            pool.memset(zero[:, :], 0.0).then_inc(consts, 1)
            pool.memset(cnt[:, :, :], 0.0).then_inc(consts, 1)
            pool.memset(epsc[:, :], EPS).then_inc(consts, 1)
            pool.iota(lane[:, :], [[1, P]], base=0, channel_multiplier=0,
                      allow_small_or_imprecise_dtypes=True).then_inc(consts, 1)
            pool.iota(tcol[:, :], [[1, TB]], base=0, channel_multiplier=TB,
                      allow_small_or_imprecise_dtypes=True).then_inc(consts, 1)
            pool.iota(recd[:, :, 4], [[1, EPT]], base=0, channel_multiplier=EPT).then_inc(consts, 1)
            pool.memset(recd[:, :, RW - 1], 0).then_inc(consts, 1)
            pool.memset(tmpl[:, :], 0).then_inc(consts, 1)
            pool.memset(tmpls[:, :], 0).then_inc(consts, 1)
            pool.memset(b2w[:, :], 0.0).then_inc(b2_clear, 1)
            pool.memset(ones_r[:, :].bitcast(F32), 1.0).then_inc(consts, 1)
            pool.wait_ge(consts, 12)
            pool.affine_select(out=ident[:, :], in_=ident[:, :], compare_op=ALU.not_equal, fill=1.0,
                               base=0, pattern=[[-1, P]], channel_multiplier=1).then_inc(consts, 1)
            pool.affine_select(out=tri[:, :], in_=ones[:, :], compare_op=ALU.is_gt, fill=0.0,
                               base=0, pattern=[[1, P]], channel_multiplier=-1).then_inc(consts, 1)
            pool.memset(tmpl[:, :].bitcast(F32).rearrange("p (t w) -> p t w", w=RW)[:, :, 2], -1.0).then_inc(tmpl_ready, 1)
            pool.memset(tmpls[:, :].bitcast(F32).rearrange("p (t w) -> p t w", w=SW)[:, :, 1], -1.0).then_inc(tmpl_ready, 1)

            def scatter(k):
                rw = WORDS[k]
                with pool.Fori(0, SCHUNKS // 2) as c:
                    for par in range(2):
                        pool.wait_ge(scat_in[k][par], c * 16 + 16)
                        pool.sem_inc(went_on, 1)
                        for j in range(SC):
                            r = scat[:, par, j * rw:(j + 1) * rw]
                            pool.indirect_dma_start(out=(r_dst, r_src)[k], in_=r, in_offset=None,
                                                    out_offset=bass.IndirectOffsetOnAxis(ap=r[:, rw - 1:rw], axis=0))\
                                .then_inc(scattered[k][par], 16)

            def gather(L, table, column, width, features=False):
                rw = WORDS[HALF[L]]
                with pool.Fori(0, TURNS) as c:
                    for j in range(BODY):
                        par, s, r = j // U, j % U, rec[:, j // U, (j % U) * rw:(j % U + 1) * rw]
                        if s == 0:
                            pool.wait_ge(rec_in[par], c * PER[L] + (BEFORE[L] + PER[L]))
                            pool.sem_inc(went_on, 1)
                            for t in range(U if features else 0):
                                pool.indirect_dma_start(
                                    out=attr[:, par * U + t, :], out_offset=None, in_=edge_attr,
                                    in_offset=bass.IndirectOffsetOnAxis(ap=rec[:, par, t * RW + 4:t * RW + 5], axis=0))\
                                    .then_inc(attr_in[par], 16)
                        pool.wait_ge(done[L], c * BODY + j + 1 + U)
                        pool.sem_inc(went_on, 1)
                        pool.indirect_dma_start(out=G[:, s, 0:width], out_offset=None, in_=table,
                                                in_offset=bass.IndirectOffsetOnAxis(ap=r[:, column:column + 1], axis=0))\
                            .then_inc(gathered[s], 16)

            def clear(L):
                pool.wait_ge(n[L - 1]["accok"], 1)
                pool.memset(accf, 0.0).then_inc(acc_clear, 1)

            pool.wait_ge(prefilled, 16 * 8)
            pool.wait_ge(tb_ready, 1)
            in_order = pool.value_load(flagi[0:1, 0:1], min_val=0, max_val=1)
            scatter(1)
            with pool.If(in_order == 0):
                scatter(0)
            pool.wait_ge(scratch_free, 1)
            pool.wait_ge(q["ev"], NB * R + 8)
            pool.memset(accf, 0.0).then_inc(acc_clear, 1)

            def stored(L):
                for par in range(2):
                    pool.wait_ge(n[L][f"sto{par}"], 16 * (NB // 2) + 16)

            for par in range(2):
                pool.wait_ge(q[f"st{par}"], 16 * NB + 16)
            gather(0, t_rel, 0, D)
            clear(1)
            pool.memset(G[:, :, D:D + 1], 1.0).then_inc(ones_in, 1)
            stored(0)
            gather(1, t_h, 0, D)
            clear(2)
            stored(1)
            with pool.If(in_order == 1):
                gather(2, t_pg, 1, 2 * D)
            with pool.Else():
                gather(2, t_pg, 1, 2 * D, features=True)
            clear(3)
            stored(2)
            gather(3, t_x3, 0, D)
            clear(4)
            stored(3)
            gather(4, t_y1, 0, D)

        @block.vector
        def _(dve):
            ch = Chain(dve, v_sem)
            V = nc.vector

            dve.wait_ge(s_ld["edges"], 16 * 7)
            dve.wait_ge(consts, 14)
            ri = [raw[:, k, :].bitcast(I32) for k in range(5)]
            sc = ind.bitcast(I32)
            V.scalar_tensor_tensor(out=recd[:, :, 0], in0=ri[0], scalar=float(R), in1=ri[2],
                                   op0=ALU.mult, op1=ALU.add)
            V.tensor_copy(recd[:, :, 1], ri[0])
            V.tensor_copy(recd[:, :, 3].bitcast(F32), raw[:, 3, :])
            V.tensor_copy(recs[:, :, 0], ri[1])
            V.tensor_copy(recd[:, :, 2].bitcast(F32), ri[1])
            ch.step(V.tensor_tensor(run, ri[1], ri[4], ALU.is_gt))
            ch.wait()
            ch.step(V.tensor_reduce(cnt[0:EPP, 0, USED:USED + 1], run, mybir.AxisListType.X, ALU.add))
            ch.step(V.tensor_scalar(sc, ri[0], P - 1, None, ALU.bitwise_and))
            ch.wait()
            ch.step(V.tensor_copy(recs[:, :, 1].bitcast(F32), sc))
            ch.wait()
            for key, r in ((1, ri[1]), (0, ri[0])):
                ch.step(V.tensor_scalar(sc, r, 7, None, ALU.arith_shift_right))
                ch.wait()
                ch.step(V.tensor_copy(blk["dst" if key else "src"], sc))
                ch.wait()
            V.memset(tj[:, :], 0.0).then_inc(raw_used, 1)

            for k, key in enumerate(("dst", "src")):
                with dve.Fori(0, USED) as d:
                    ch.enter(d, 1)
                    ch.wait()
                    ch.step(V.tensor_scalar(ind, blk[key], lane[0:EPP, bass.ds(d, 1)], None, ALU.is_equal, ALU.add,
                                            accum_out=cnt[0:EPP, k, bass.ds(d, 1)]))
                    ch.leave(USED)
                ch.wait()
                dve.sem_inc(counted, 1)
            dve.wait_ge(based, 1)
            total, before, nt, end, first, base, shift = (blks[:, i, :] for i in range(7))
            for k in range(2):
                ch.step(V.tensor_copy(total[:, 0:USED + 1], ps[7][:, (2 * k + 1) * P:(2 * k + 1) * P + USED + 1]))
                ch.step(V.tensor_copy(before[:, 0:USED], ps[7][:, 2 * k * P:2 * k * P + USED]))
                ch.wait()
                u = slice(0, USED)
                ch.step(V.tensor_scalar(blki[:, u], total[:, u], float(P - 1), None, ALU.add))
                ch.wait()
                ch.step(V.tensor_scalar(blki[:, u], blki[:, u], 7, None, ALU.arith_shift_right))
                ch.wait()
                ch.step(V.tensor_copy(nt[:, u], blki[:, u]))
                ch.wait()
                ch.step(V.tensor_tensor_scan(end[:, u], ones[:, u], nt[:, u], 0.0, ALU.mult, ALU.add))
                ch.wait()
                ch.step(V.tensor_tensor(first[:, u], end[:, u], nt[:, u], ALU.subtract))
                ch.wait()
                ch.step(V.scalar_tensor_tensor(out=base[:, u], in0=first[:, u], scalar=float(P), in1=before[:, u],
                                               op0=ALU.mult, op1=ALU.add))
                ch.wait()
                ch.step(V.tensor_scalar(blks[:, 6 + k, u], base[:, u], -1.0, None, ALU.add))
                ch.wait()
                m = slice(0, USED - 1)
                for j in range(TB):
                    ch.step(V.tensor_scalar(tj[:, m], end[:, m], tcol[:, j:j + 1], None, ALU.is_le, ALU.add,
                                            accum_out=tbf[:, k, j:j + 1]))
                    ch.wait()
                if k == 0:
                    ch.step(V.tensor_scalar(flag[:, 0:1], total[:, USED:USED + 1], 0.0, None, ALU.is_equal))
                    ch.step(V.scalar_tensor_tensor(out=base[:, u], in0=nt[:, u], scalar=-float(P), in1=total[:, u],
                                                   op0=ALU.mult, op1=ALU.add))
                    ch.wait()
                    ch.step(V.tensor_scalar(base[:, u], base[:, u], flag[:, 0:1], None, ALU.mult))
                    ch.step(V.tensor_copy(flagi[:, :], flag[:, 0:1]))
                    ch.step(V.tensor_scalar(tbf[:, 3, :], tbf[:, 0, :], float(P), None, ALU.mult))
                    ch.wait()
                    for j in range(TB):
                        ch.step(V.tensor_scalar(tj[:, m], end[:, m], tcol[:, j:j + 1], None, ALU.is_le))
                        ch.wait()
                        ch.step(V.tensor_tensor(tj[:, m], tj[:, m], base[:, m], ALU.mult))
                        ch.wait()
                        ch.step(V.tensor_reduce(tbf[:, 2, j:j + 1], tj[:, m], mybir.AxisListType.X, ALU.add))
                        ch.wait()
                    ch.step(V.scalar_tensor_tensor(out=tbf[:, 2, :], in0=tcol[:, :], scalar=float(P), in1=tbf[:, 2, :],
                                                   op0=ALU.mult, op1=ALU.add))
            ch.wait()
            ch.step(V.tensor_copy(tbi[:, :, :], tbf[:, 0:3, :]))
            ch.wait()
            dve.sem_inc(tb_ready, 1)

            def find_slots(k, key, ch):
                with dve.Fori(0, USED) as d:
                    ch.enter(d, 3)
                    ch.wait()
                    ch.step(V.tensor_scalar(ind, blk[key], lane[0:EPP, bass.ds(d, 1)], None, ALU.is_equal))
                    ch.wait()
                    ch.step(V.tensor_tensor_scan(run, ind, zero[0:EPP, 0:1].to_broadcast([EPP, EPT]),
                                                 blks[0:EPP, 6 + k, bass.ds(d, 1)], ALU.add, ALU.add))
                    ch.wait()
                    dve.sem_inc(went_on, 1)
                    ch.step(V.copy_predicated(slot, ind.bitcast(I32), run))
                    ch.leave(USED)
                ch.wait()
                if k == 0:
                    ch.step(V.tensor_copy(recd[:, :, RW - 1], slot))
                else:
                    si, hi = ind.bitcast(I32), run.bitcast(I32)
                    ch.step(V.tensor_copy(si, slot))
                    ch.wait()
                    ch.step(V.tensor_scalar(hi, si, 7, None, ALU.arith_shift_right))
                    ch.step(V.tensor_scalar(slot.bitcast(I32), si, P - 1, None, ALU.bitwise_and))
                    ch.wait()
                    ch.step(V.scalar_tensor_tensor(out=recs[:, :, SW - 1], in0=slot.bitcast(I32), scalar=float(TILES),
                                                   in1=hi, op0=ALU.mult, op1=ALU.add))
                ch.wait()
                dve.sem_inc(slots_ready[k], 1)

            find_slots(1, "src", ch)
            in_order = dve.value_load(flagi[0:1, 0:1], min_val=0, max_val=1)
            with dve.If(in_order == 0):
                find_slots(0, "dst", Chain(dve, v_branch))
            dve.sem_inc(scratch_free, 1)

            dve.wait_ge(s_ld["parts"], 16 * 7)

            def part(raw_ap, high, low):
                ch.step(V.tensor_copy(high, raw_ap))
                ch.wait()
                ch.step(V.tensor_tensor(low, raw_ap, high.bitcast(F32), ALU.subtract))

            part(st[:, 0, :], weh[:, :], wel[:, :])
            part(st[:, 1, :].rearrange("p (c o) -> p c o", c=KC), w2h[:, :, :], w2l[:, :, :])
            b2t = ts[0:64, 0, :]
            ch.step(V.memset(b2h[:, :].bitcast(F32), 0.0))
            ch.wait()
            ch.step(V.tensor_copy(b2h[:, :], b2w[:, :]))
            ch.wait()
            ch.step(V.tensor_tensor(b2t, b2w[:, :], b2h[:, :].bitcast(F32), ALU.subtract))
            ch.wait()
            ch.step(V.tensor_copy(b2h[32:33, :], b2t[32:33, :]))
            ch.wait()

            blk_regs = [dve.alloc_register(f"blk{j}") for j in range(BODY)]

            def load_blocks(k, c):
                dve.load(blk_regs, tbrow[0:1, k, bass.ds(c * BODY, BODY)])

            def make_hot(L, T, j, c):
                rw = WORDS[HALF[L]]
                par, s = j // U, j % U
                if s == 0:
                    dve.wait_ge(rec_in[par], c * PER[L] + (BEFORE[L] + PER[L]))
                    if HALF[L] == 0:
                        dst_of = rec[:, par, :].bitcast(F32).rearrange("p (t w) -> p t w", w=RW)[:, :, 2]
                        V.tensor_tensor(local[:, par, :], dst_of, node0[:, bass.ds(c * BODY + par * U, U)], ALU.subtract)\
                            .then_inc(located, 1)
                        turns = TURNS * 2 * (L // 2)
                        dve.wait_ge(located, c * 2 + (par + 1 + turns))
                r = rec[:, par, s * rw:(s + 1) * rw].bitcast(F32)
                node = local[:, par, s:s + 1] if HALF[L] == 0 else r[:, 1:2]
                if L == 0:
                    V.tensor_scalar(onehot[:, s, :], lane[:, :], node, r[:, 3:4], ALU.is_equal, ALU.mult)\
                        .then_inc(hot[L], 1)
                else:
                    V.tensor_scalar(onehot[:, s, :], lane[:, :], node, None, ALU.is_equal).then_inc(hot[L], 1)

            def add_tile(L, T, j, width, bank):
                b = dve.snap(blk_regs[j], min_val=0, max_val=USED - 1)
                dve.wait_ge(summed[L], T + 1)
                dve.wait_ge(done[L], T + BODY)
                a = acc_(b, width)
                V.tensor_tensor(a, a, bank[:, 0:width], ALU.add).then_inc(done[L], 1)

            def edge_adds(L, width):
                dve.wait_ge(acc_clear, L + 1)
                dve.wait_ge(tb_back, 64)
                LAG = 3
                with dve.Fori(0, TURNS) as c:
                    load_blocks(HALF[L], c)
                    for j in range(BODY + LAG):
                        if j < BODY:
                            make_hot(L, c * BODY + j, j, c)
                        if j >= LAG:
                            add_tile(L, c * BODY + j - LAG, j - LAG, width, ps[(j - LAG) % 4])

            def attr_low(c, jj):
                T, o = c * BODY + jj, jj % 2
                dve.wait_ge(e["atc"], T + 1)
                V.tensor_tensor(attrT[DE:P, o, :], ps[0][0:DE, 0:P], attrT[0:DE, o, :].bitcast(F32), ALU.subtract)\
                    .then_inc(e["atl"], 1)

            def hidden_low(c, jj):
                T, o = c * BODY + jj, jj % 2
                dve.wait_ge(e["relu"], T + 1)
                V.scalar_tensor_tensor(out=HTl[:, o, :, :].rearrange("p c n -> p (c n)"), in0=ps[1 + o][:, 0:D],
                                       scalar=0.0, in1=HTh[:, o, :, :].rearrange("p c n -> p (c n)").bitcast(F32),
                                       op0=ALU.max, op1=ALU.subtract).then_inc(e["htl"], 1)

            def gate_sum(c, jj):
                T, o = c * BODY + jj, jj % 2
                dve.wait_ge(e["gp"], T + 3)
                dve.wait_ge(e["sig"], T + 1)
                V.tensor_tensor(gs[:, o, :], ps[3 + o][:, 0:D], G[:, jj % U, D:2 * D], ALU.add).then_inc(e["gs"], 1)

            def message(c, jj):
                T, o = c * BODY + jj, jj % 2
                dve.wait_ge(e["sig"], T + 3)
                dve.wait_ge(e["core"], T + 3)
                V.tensor_tensor(msg[:, o, :], ps[5 + o][:, 0:D], sg[:, o, :], ALU.mult).then_inc(e["msg"], 1)

            def edge2_turn(c, first=False, last=False):
                if first:
                    load_blocks(0, c)
                for j in range(BODY):
                    if j == 2 and not first:
                        load_blocks(0, c)
                    make_hot(2, c * BODY + j, j, c)
                    if not (last and j == BODY - 1):
                        attr_low(c, j + 1)
                    hidden_low(c, j)
                    gate_sum(c, j)
                    if not first or j >= 1:
                        message(c, j - 1)
                    if not first or j >= 2:
                        add_tile(2, c * BODY + (j - 2), (j - 2) % BODY, D, ps[7])

            def edge2():
                dve.wait_ge(acc_clear, 3)
                attr_low(0, 0)
                edge2_turn(0, first=True)
                with dve.Fori(1, TURNS - 1) as c:
                    edge2_turn(c)
                edge2_turn(TURNS - 1, last=True)
                message(TURNS - 1, BODY - 1)
                for j in (BODY - 2, BODY - 1):
                    add_tile(2, (TURNS - 1) * BODY + j, j, D, ps[7])

            def finish_stats(L, which):
                ch.wait()
                s = stats[:, :, :]
                ch.step(V.tensor_tensor(lt[:, 0, :], s[:, :, 1], s[:, :, 4], ALU.add))
                ch.step(V.tensor_tensor(lt[:, 1, :], s[:, :, 1], s[:, :, 4], ALU.subtract))
                ch.step(V.tensor_tensor(rstd[:, :], s[:, :, 2], s[:, :, 5], ALU.add))
                ch.wait()
                ch.step(V.tensor_scalar(mean[:, :], lt[:, 0, :], 0.5, None, ALU.mult))
                ch.step(V.tensor_tensor(lt[:, 1, :], lt[:, 1, :], lt[:, 1, :], ALU.mult))
                ch.step(V.tensor_scalar(rstd[:, :], rstd[:, :], 1.0 / D, None, ALU.mult))
                ch.wait()
                ch.step(V.scalar_tensor_tensor(out=lt[:, 0, :], in0=lt[:, 1, :], scalar=0.25, in1=rstd[:, :],
                                               op0=ALU.mult, op1=ALU.add))
                ch.wait()
                dve.sem_inc(n[L]["var"], 1)
                dve.wait_ge(n[L]["std"], which + 1)
                ch.step(V.reciprocal(rstd[:, :], lt[:, 1, :]))
                ch.wait()

            def stat(b, of):
                V_out = stats[:, bass.ds(b, 1), :].rearrange("p a w -> p (a w)")
                ch.step(V.bn_stats(V_out, of))

            def normed(dst_ap, of, b):
                return V.tensor_scalar(dst_ap, of, mean[:, bass.ds(b, 1)], rstd[:, bass.ds(b, 1)],
                                       ALU.subtract, ALU.mult)

            def residual(L, relu):
                with dve.Fori(0, NB) as b:
                    ch.enter(b, 2)
                    if relu:
                        ch.step(V.scalar_tensor_tensor(out=X_(b), in0=acc_(b), scalar=0.0, in1=X_(b),
                                                       op0=ALU.max, op1=ALU.add))
                    else:
                        ch.step(V.tensor_tensor(X_(b), acc_(b), X_(b), ALU.add))
                    ch.wait()
                    stat(b, X_(b))
                    ch.leave(NB)
                ch.wait()

            def normalise_and_bias(L, width, bias):
                S = n[L]
                with dve.Fori(0, NB // 2) as c:
                    for par in range(2):
                        T = c * 2 + par
                        dve.wait_ge(S["xsc"], T + 1)
                        dve.wait_ge(S["tp"], T + 1)
                        normed(xs[:, par, :], X_(T), T).then_inc(S["xs"], 1)
                    for par in range(2):
                        T = c * 2 + par
                        dve.wait_ge(S["mm"], T + 3)
                        dve.wait_ge(S[f"sto{par}"], c * 16 + 16)
                        V.tensor_tensor(st[:, par, 0:width], ps[par][:, 0:width], bias, ALU.add).then_inc(S["st"], 1)

            edge_adds(0, D)
            dve.wait_ge(done[0], TILES + BODY)
            dve.wait_ge(s_ld["x"], 32)
            dve.wait_ge(s_ld["late"], 16 * LATE)
            residual(0, True)
            finish_stats(0, 0)
            dve.sem_inc(n[0]["accok"], 1)
            normalise_and_bias(0, D, rows["b_l1"][:, :])

            edge_adds(1, AW)
            dve.wait_ge(done[1], TILES + BODY)
            dve.wait_ge(n[0]["xsc"], NB + 2)
            residual(1, False)
            ch.step(V.tensor_scalar(rdeg[:, :], acc[:, :, D], 1.0, None, ALU.max))
            ch.wait()
            ch.step(V.reciprocal(rdeg[:, :], rdeg[:, :]))
            finish_stats(1, 0)
            dve.sem_inc(n[1]["accok"], 1)
            normalise_and_bias(1, 2 * D, bpg[:, :])

            edge2()
            dve.wait_ge(done[2], TILES + BODY)
            dve.wait_ge(n[1]["xsc"], NB + 2)
            with dve.Fori(0, NB) as b:
                ch.enter(b, 2)
                ch.step(V.tensor_tensor(acc_(b), acc_(b), X_(b), ALU.add))
                ch.wait()
                stat(b, acc_(b))
                ch.leave(NB)
            finish_stats(2, 0)
            with dve.Fori(0, NB) as b:
                ch.enter(b, 5)
                ch.step(normed(acc_(b), acc_(b), b))
                ch.wait()
                ch.step(V.tensor_tensor(acc_(b), acc_(b), rows["gamma"][:, :], ALU.mult))
                ch.wait()
                ch.step(V.tensor_tensor(acc_(b), acc_(b), rows["beta"][:, :], ALU.add))
                ch.wait()
                ch.step(V.tensor_tensor(acc_(b), acc_(b), X_(b), ALU.add))
                ch.wait()
                stat(b, acc_(b))
                ch.leave(NB)
            finish_stats(2, 1)
            with dve.Fori(0, NB // 2) as c:
                for par in range(2):
                    T = c * 2 + par
                    dve.wait_ge(n[2]["xsc"], T + 1)
                    dve.wait_ge(n[2][f"sto{par}"], c * 16 + 16)
                    normed(xs[:, par, :], acc_(T), T).then_inc(n[2]["xs"], 1)
            dve.wait_ge(n[2]["xs"], NB)
            dve.sem_inc(n[2]["accok"], 1)

            for L, bias, g, be in ((3, "b_a", "g_a", "be_a"), (4, "b_b", "g_b", "be_b")):
                S = n[L]
                edge_adds(L, D)
                dve.wait_ge(done[L], TILES + BODY)
                dve.wait_ge(n[L - 1]["xsc"], NB + 2)
                with dve.Fori(0, NB // 2) as c:
                    ch.enter(c, 2)
                    for par in range(2):
                        T = c * 2 + par
                        dve.wait_ge(S["tp"], T + 1)
                        V.scalar_tensor_tensor(out=xs[:, par, :], in0=acc_(T), scalar=rdeg[:, bass.ds(T, 1)],
                                               in1=X_(T), op0=ALU.mult, op1=ALU.add).then_inc(S["xs"], 1)
                    for par in range(2):
                        T = c * 2 + par
                        dve.wait_ge(S["mm"], T + 3)
                        V.tensor_tensor(acc_(T), ps[par][:, 0:D], rows[bias][:, :], ALU.add).then_inc(S["st"], 1)
                        dve.wait_ge(S["st"], T + 3)
                        stat(T, acc_(T))
                    ch.leave(NB // 2)
                finish_stats(L, 0)
                with dve.Fori(0, NB // 2) as c:
                    ch.enter(c, 4 if L == 3 else 8)
                    for par in range(2):
                        T = c * 2 + par
                        t = ts[:, par, :]
                        dve.wait_ge(S["ys"], T + 1)
                        ch.step(normed(t, acc_(T), T))
                        ch.wait()
                        ch.step(V.tensor_tensor(t, t, rows[g][:, :], ALU.mult))
                        ch.wait()
                        V.tensor_tensor(t, t, rows[be][:, :], ALU.add).then_inc(S["ts"], 1)
                    for par in range(2):
                        T = c * 2 + par
                        dve.wait_ge(S["sg"], T + 1)
                        if L == 3:
                            dve.wait_ge(S["xsc"], T + 1)
                            dve.wait_ge(S[f"sto{par}"], c * 16 + 16)
                            V.tensor_tensor(st[:, par, 0:D], ts[:, par, :], sg[:, par, :], ALU.mult).then_inc(S["ys"], 1)
                        else:
                            V.tensor_tensor(X_(T), ts[:, par, :], sg[:, par, :], ALU.mult).then_inc(S["ys"], 1)
                            dve.wait_ge(S["ys"], T + 3)
                            dve.wait_ge(x3_in[par], c * 16 + 16)
                            ch.step(V.tensor_tensor(X_(T), X_(T), xs[:, par, :], ALU.add))
                            ch.wait()
                            stat(T, X_(T))
                            ch.wait()
                            dve.sem_inc(x3_used, 1)
                    ch.leave(NB // 2)
                if L == 3:
                    dve.wait_ge(S["ys"], NB + 2)
                    dve.sem_inc(S["accok"], 1)
            finish_stats(4, 1)
            with dve.Fori(0, NB // 2) as c:
                for par in range(2):
                    T = c * 2 + par
                    dve.wait_ge(n[4][f"sto{par}"], c * 16 + 16)
                    normed(st[:, par, 0:D], X_(T), T).then_inc(out_ready, 1)

        @block.scalar
        def _(act):
            A = nc.scalar

            def into_X(sem_, value, T, of):
                act.wait_ge(sem_, value)
                act.sem_inc(went_on, 1)
                return A.activation(X_(T), of, ACT.Copy)

            act.wait_ge(s_ld["x"], 32)
            act.wait_ge(raw_used, 1)
            trows = t_rel.rearrange("(m r) d -> m (r d)", r=R)
            with act.Fori(0, NB // 2) as c:
                for par in range(2):
                    T = c * 2 + par
                    act.wait_ge(q["xt"], T + 1)
                    act.sem_inc(went_on, 1)
                    A.activation(xs[:, par, :], X_(T), ACT.Copy).then_inc(q["xs"], 1)
                    act.wait_ge(q["xt"], T + 3)
                    A.activation(xT[:, par, :, :], ps[4 + par][:, 0:D].rearrange("p (c n) -> p c n", c=KC), ACT.Copy)\
                        .then_inc(q["xtc"], 1)
                    act.wait_ge(q["pg"], T + 1)
                    A.activation(gate[:, par, :], ps[6][:, 0:R], ACT.Sigmoid).then_inc(q["gate"], 1)
                    act.wait_ge(q["gate"], T + 2)
                    for g in range(R // 2):
                        h = g // 4
                        act.wait_ge(q["pr"], T * (R // 2) + (g + 1))
                        if g % 4 == 0:
                            act.wait_ge(q[f"st{h}"], T * 16 + 16)
                        for r in range(2):
                            A.activation(stage[:, h, ((g % 4) * 2 + r) * D:((g % 4) * 2 + r + 1) * D],
                                         ps[g % 4][:, r * D:(r + 1) * D], ACT.Copy,
                                         scale=gate[:, par, 2 * g + r:2 * g + r + 1]).then_inc(q["ev"], 1)
                        if g % 4 == 3:
                            act.wait_ge(q["ev"], T * R + (8 * (h + 1) + 8))
                            act.dma_start(trows[bass.ds(T * P, P), h * 8 * D:(h + 1) * 8 * D], stage[:, h, :])\
                               .then_inc(q[f"st{h}"], 16)

            def std(L, which):
                act.wait_ge(n[L]["var"], which + 1)
                A.activation(lt[:, 1, :], lt[:, 0, :], ACT.Sqrt, bias=epsc[:, 0:1]).then_inc(n[L]["std"], 1)

            def transposed(L, T, par):
                S = n[L]
                act.wait_ge(S["tp"], T + 3)
                act.wait_ge(S["mm"], T + 1)
                A.activation(xT[:, par, :, :], ps[6 + par][:, 0:D].rearrange("p (c n) -> p c n", c=KC), ACT.Copy)\
                    .then_inc(S["tpc"], 1)

            def node_plain(L):
                std(L, 0)
                with act.Fori(0, NB // 2) as c:
                    for par in range(2):
                        T = c * 2 + par
                        into_X(n[L]["xs"], T + 1, T, xs[:, par, :]).then_inc(n[L]["xsc"], 1)
                        transposed(L, T, par)

            node_plain(0)
            node_plain(1)

            def attr_high(T, jj):
                act.wait_ge(e["at"], T + 1)
                act.wait_ge(e["gp"], T + 1)
                A.activation(attrT[0:DE, jj % 2, :], ps[0][0:DE, 0:P], ACT.Copy).then_inc(e["atc"], 1)

            def act_step(T, j, last=False):
                if not last:
                    attr_high(T + 1, j + 1)
                act.wait_ge(e["ht"], T + 1)
                act.wait_ge(e["core"], T + 1)
                A.activation(HTh[:, j % 2, :, :], ps[1 + j % 2][:, 0:D].rearrange("p (c n) -> p c n", c=KC), ACT.Relu)\
                    .then_inc(e["relu"], 1)
                act.wait_ge(e["gs"], T + 3)
                act.wait_ge(e["msg"], T + 1)
                A.activation(sg[:, j % 2, :], gs[:, j % 2, :], ACT.Sigmoid).then_inc(e["sig"], 1)

            attr_high(0, 0)
            with act.Fori(0, TURNS - 1) as c:
                for j in range(BODY):
                    act_step(c * BODY + j, j)
            for j in range(BODY):
                act_step((TURNS - 1) * BODY + j, j, j == BODY - 1)

            std(2, 0)
            std(2, 1)
            with act.Fori(0, NB // 2) as c:
                for par in range(2):
                    T = c * 2 + par
                    into_X(n[2]["xs"], T + 1, T, xs[:, par, :]).then_inc(n[2]["xsc"], 1)

            for L in (3, 4):
                S = n[L]
                with act.Fori(0, NB // 2) as c:
                    for par in range(2):
                        transposed(L, c * 2 + par, par)
                std(L, 0)
                with act.Fori(0, NB // 2) as c:
                    for par in range(2):
                        T = c * 2 + par
                        act.wait_ge(S["ts"], T + 1)
                        act.wait_ge(S["ys"], T + 1)
                        A.activation(sg[:, par, :], ts[:, par, :], ACT.Sigmoid).then_inc(S["sg"], 1)
                    if L == 3:
                        for par in range(2):
                            T = c * 2 + par
                            into_X(S["ys"], T + 3, T, st[:, par, 0:D]).then_inc(S["xsc"], 1)
            std(4, 1)

        @block.tensor
        def _(pe):
            T_ = nc.tensor

            pe.wait_ge(consts, 14)
            pe.wait_ge(counted, 2)
            for k in range(2):
                for h, m in enumerate((tri, ones)):
                    last = T_.matmul(ps[7][:, (2 * k + h) * P:(2 * k + h) * P + USED + 1], m[0:EPP, :],
                                     cnt[0:EPP, k, 0:USED + 1], start=True, stop=True)
            last.then_inc(based, 1)

            pe.wait_ge(s_ld["wgate"], 16)
            pe.wait_ge(s_ld["wrel"], 32)
            with pe.Fori(0, NB // 2) as c:
                for par in range(2):
                    T = c * 2 + par
                    pe.wait_ge(q["xs"], T + 1)
                    pe.wait_ge(q["xtc"], T + 1)
                    for k in range(KC):
                        last = T_.transpose(ps[4 + par][:, k * P:(k + 1) * P], xs[:, par, k * P:(k + 1) * P], ident[:, :])
                    last.then_inc(q["xt"], 1)
                    pe.wait_ge(q["xtc"], T + 3)
                    pe.wait_ge(q["gate"], T + 1)
                    for k in range(KC):
                        last = T_.matmul(ps[6][:, 0:R], xT[:, par, k, :], wgate[:, k, :], start=k == 0, stop=k == KC - 1)
                    last.then_inc(q["pg"], 1)
                    for g in range(R // 2):
                        pe.wait_ge(q["ev"], T * R + (2 * g + 2))
                        for k in range(KC):
                            last = T_.matmul(ps[g % 4][:, :], xT[:, par, k, :], wrel[:, k, g * 2 * D:(g + 1) * 2 * D],
                                             start=k == 0, stop=k == KC - 1)
                        last.then_inc(q["pr"], 1)

            def rows_in(L, c, jj):
                pe.wait_ge(gathered[jj % U], (c * 2 + (jj // U + 1 + 2 * TURNS * L)) * 16)

            def edge_sums(L, width):
                with pe.Fori(0, TURNS) as c:
                    for j in range(BODY):
                        pe.wait_ge(hot[L], c * BODY + j + 1)
                        rows_in(L, c, j)
                        pe.wait_ge(done[L], c * BODY + j + (1 + BODY - 4))
                        T_.matmul(ps[j % 4][:, 0:width], onehot[:, j % U, :], G[:, j % U, 0:width],
                                  start=True, stop=True).then_inc(summed[L], 1)

            def transposes(L, T, par):
                S = n[L]
                pe.wait_ge(S["xs"], T + 1)
                pe.wait_ge(S["tpc"], T + 1)
                for k in range(KC):
                    last = T_.transpose(ps[6 + par][:, k * P:(k + 1) * P], xs[:, par, k * P:(k + 1) * P], ident[:, :])
                last.then_inc(S["tp"], 1)

            def products(L, weights, width):
                S = n[L]
                with pe.Fori(0, NB // 2) as c:
                    for par in range(2):
                        transposes(L, c * 2 + par, par)
                    for par in range(2):
                        T = c * 2 + par
                        pe.wait_ge(S["tpc"], T + 3)
                        pe.wait_ge(S["st"], T + 1)
                        for k in range(KC):
                            last = T_.matmul(ps[par][:, 0:width], xT[:, par, k, :], weights[:, k, :],
                                             start=k == 0, stop=k == KC - 1)
                        last.then_inc(S["mm"], 1)

            edge_sums(0, D)
            pe.wait_ge(s_ld["late"], 16 * LATE)
            products(0, wl1, D)
            pe.wait_ge(ones_in, 1)
            edge_sums(1, AW)
            products(1, wpg, 2 * D)

            def A(c, jj):
                pe.wait_ge(attr_in[jj // U % 2], (c + (jj // BODY + 1)) * (16 * U))
                pe.wait_ge(e["atl"], c * BODY + (jj + 1))
                pe.sem_inc(went_on, 1)
                T_.transpose(ps[0][0:DE, 0:P], attr[:, jj % BODY, :], ident[:, :]).then_inc(e["at"], 1)

            def B(c, jj):
                T, s = c * BODY + jj, jj % U
                rows_in(2, c, jj)
                pe.wait_ge(e["atl"], T + 2)
                pe.wait_ge(e["htl"], T + 1)
                for k in range(KC):
                    o = ps[1 + jj % 2][:, k * P:(k + 1) * P]
                    T_.matmul(o, G[:, s, k * P:(k + 1) * P], ident[:, :], is_transpose=True, start=True, stop=False)
                    T_.matmul(o, weh[:, k * P:(k + 1) * P], attrT[:, jj % 2, :], start=False, stop=False)
                    last = T_.matmul(o, wel[:, k * P:(k + 1) * P], attrT[:, jj % 2, :], start=False, stop=True)
                last.then_inc(e["ht"], 1)
                pe.wait_ge(e["gs"], T + 1)
                o = ps[3 + jj % 2][:, 0:D]
                T_.matmul(o, attrT[:, jj % 2, :], weh[:, D:2 * D], start=True, stop=False)
                T_.matmul(o, attrT[:, jj % 2, :], wel[:, D:2 * D], start=False, stop=True).then_inc(e["gp"], 1)

            def C(c, jj):
                T = c * BODY + jj
                pe.wait_ge(e["htl"], T + 3)
                pe.wait_ge(e["msg"], T + 1)
                o = ps[5 + jj % 2][:, 0:D]
                for k in range(KC):
                    for n_, (a, b) in enumerate(((HTh, w2h), (HTh, w2l), (HTl, w2h))):
                        T_.matmul(o, a[:, jj % 2, k, :], b[:, k, :], start=k == 0 and n_ == 0, stop=False)
                T_.matmul(o, ones_r[:, :], b2h[:, :], start=False, stop=True).then_inc(e["core"], 1)

            def D_(c, jj):
                T = c * BODY + jj
                pe.wait_ge(hot[2], T + 1)
                pe.wait_ge(e["msg"], T + 3)
                pe.wait_ge(done[2], T + BODY)
                T_.matmul(ps[7][:, 0:D], onehot[:, jj % U, :], msg[:, jj % 2, :], start=True, stop=True)\
                    .then_inc(summed[2], 1)

            def pe_turn(c, first=False, last=False):
                for j in range(BODY):
                    if not (last and j == BODY - 1):
                        A(c, j + 1)
                    B(c, j)
                    if not first or j >= 1:
                        C(c, j - 1)
                    if not first or j >= 2:
                        D_(c, j - 2)

            A(0, 0)
            pe_turn(0, first=True)
            with pe.Fori(1, TURNS - 1) as c:
                pe_turn(c)
            pe_turn(TURNS - 1, last=True)
            C(TURNS - 1, BODY - 1)
            D_(TURNS - 1, BODY - 2)
            D_(TURNS - 1, BODY - 1)

            for L in (3, 4):
                edge_sums(L, D)
                products(L, wab[:, L - 3], D)


_OUT = ((N, D), "float32")


def kernel(x, src, dst, edge_attr_64, edge_type_16, edge_weight1, L0_gnn_weight, L0_gnn_gate_weight,
           L1_gnn_W, L1_gnn_b, L2_gnn_W1, L2_gnn_b1, L2_gnn_W2, L2_gnn_b2, L2_gnn_Wg, L2_gnn_bg,
           L2_gnn_gamma, L2_gnn_beta, L3_gnn_W0, L3_gnn_b0, L3_gnn_g0, L3_gnn_beta0, L3_gnn_W1,
           L3_gnn_b1, L3_gnn_g1, L3_gnn_beta1):
    import numpy as np
    import concourse.bacc as bacc
    from concourse.bass_utils import run_bass_kernel_spmd

    given = [
        ("x", x), ("src", src), ("dst", dst), ("edge_attr", edge_attr_64), ("edge_type", edge_type_16),
        ("edge_weight", edge_weight1), ("w_rel", L0_gnn_weight),
        ("w_gate", np.asarray(L0_gnn_gate_weight)[:, :, 0].T), ("w_l1", np.asarray(L1_gnn_W).T), ("b_l1", L1_gnn_b),
        ("w1", L2_gnn_W1), ("b1", L2_gnn_b1), ("w2", L2_gnn_W2), ("b2", L2_gnn_b2), ("wg", L2_gnn_Wg), ("bg", L2_gnn_bg),
        ("gamma", L2_gnn_gamma), ("beta", L2_gnn_beta),
        ("w_a", np.asarray(L3_gnn_W0).T), ("b_a", L3_gnn_b0), ("g_a", L3_gnn_g0), ("be_a", L3_gnn_beta0),
        ("w_b", np.asarray(L3_gnn_W1).T), ("b_b", L3_gnn_b1), ("g_b", L3_gnn_g1), ("be_b", L3_gnn_beta1),
    ]
    edge_attr = np.asarray(edge_attr_64)
    given[3] = ("edge_attr", np.concatenate([edge_attr, np.zeros((SLOTS - E, DE), edge_attr.dtype)]))
    nc = bacc.Bacc("TRN2", target_bir_lowering=False, num_devices=1)
    arrays, args = {}, {}
    for name, a in given:
        a = np.ascontiguousarray(a)
        arrays[f"in_{name}"] = a
        args[name] = nc.dram_tensor(f"in_{name}", a.shape, mybir.dt.from_np(a.dtype), kind="ExternalInput").ap()
    args["out"] = nc.dram_tensor("out_0", _OUT[0], mybir.dt.from_np(np.dtype(_OUT[1])), kind="ExternalOutput").ap()
    program(nc, **args)
    r = run_bass_kernel_spmd(nc, [arrays], core_ids=[0])
    return r.results[0]["out_0"]
```

```python
from contextlib import ExitStack

import concourse.bass as bass
from concourse import mybir

ALU = mybir.AluOpType
ACT = mybir.ActivationFunctionType
F32 = mybir.dt.float32
I32 = mybir.dt.int32
R32 = mybir.dt.float32r

P = 128
N, D = 6250, 256
E, DE, R = 100000, 64, 16
KC = D // P
NB = 50
FULL = N // P
TAIL = N - FULL * P
EPP = 125
EPT = E // EPP
USED = FULL + 1
TILES = 832
SLOTS = TILES * P
U = 8
BODY = 2 * U
CH = 4
RING = BODY // CH
TURNS = TILES // BODY
SC = 16
SCHUNKS = EPT // SC
MORE_BLOCKS = 9
SPLIT = (0, 5, 20, 22, SCHUNKS // 2)
RW = 6
SW = 3
NI = 5
MS = 4
SUM_LAG = 4
LOW_LAG = 5
LATE = 12
AW = D + 1
EPS = 1e-5
TB = 7
assert USED % 2 == 1 and NB % NI == 0 and NB % 2 == 0
assert TILES * P >= E + USED * (P - 1) and TILES % BODY == 0 and EPT % (2 * SC) == 0


class Chain:

    def __init__(self, eng, sem):
        self.eng, self.sem, self.base, self.n = eng, sem, 0, 0

    def step(self, ins):
        ins.then_inc(self.sem, 1)
        self.n += 1

    def wait(self):
        self.eng.wait_ge(self.sem, self.base + self.n)

    def wait_but_one(self):
        self.eng.wait_ge(self.sem, self.base + self.n - 1)

    def wait_for(self, k):
        self.eng.wait_ge(self.sem, self.base + k)

    def enter(self, i, per):
        self.outer, self.per = self.base + self.n, per
        self.base, self.n = self.outer + i * per, 0

    def leave(self, turns):
        assert self.n == self.per, (self.n, self.per)
        self.base, self.n = self.outer + turns * self.per, 0


def program(nc, x, src, dst, edge_attr, edge_type, edge_weight, w_rel, w_gate, w_l1, b_l1,
            w1, b1, w2, b2, wg, bg, gamma, beta, w_a, b_a, g_a, be_a, w_b, b_b, g_b, be_b, out):
    ctx = ExitStack()
    with ctx:
        def sb(name, shape, dt=F32):
            return ctx.enter_context(nc.sbuf_tensor(name, shape, dt))

        def sem(name):
            return ctx.enter_context(nc.semaphore(name))

        t_rel = nc.dram_tensor("t_rel", (NB * P * R, D), F32).ap()
        t_h = nc.dram_tensor("t_h", (NB * P, D), F32).ap()
        t_pg = nc.dram_tensor("t_pg", (NB * P, 2 * D), F32).ap()
        t_x3 = nc.dram_tensor("t_x3", (NB * P, D), F32).ap()
        t_y1 = nc.dram_tensor("t_y1", (NB * P, D), F32).ap()
        r_dst = nc.dram_tensor("r_dst", (SLOTS, RW), I32).ap()
        r_src = nc.dram_tensor("r_src", (SLOTS, SW), I32).ap()
        d_tb = nc.dram_tensor("d_tb", (3, TB * P), I32).ap()
        d_tf = nc.dram_tensor("d_tf", (1, TB * P), F32).ap()

        X = sb("X", [P, NB, D])
        acc = sb("acc", [P, NB, AW])
        accf = acc[:, :, :].rearrange("p b w -> p (b w)")
        wrel = accf[:, 0:KC * R * D].rearrange("p (c n) -> p c n", c=KC)
        o = KC * R * D
        blk = {k: accf[0:EPP, o + n * EPT:o + (n + 1) * EPT] for n, k in enumerate(("dst", "src"))}
        ind, run, slot = (accf[0:EPP, o + n * EPT:o + (n + 1) * EPT] for n in (2, 3, 4))
        arena = sb("arena", [P, 4096])
        stage = arena[:, :].rearrange("p (s n) -> p s n", s=2)
        raw = arena[0:EPP, 0:5 * EPT].rearrange("p (k t) -> p k t", k=5)
        G = arena[:, :].rearrange("p (s n) -> p s n", s=U)
        early = sb("early", [P, EPT * RW])
        recd = early[0:EPP, :].bitcast(I32).rearrange("p (t w) -> p t w", w=RW)
        recs = sb("recs", [P, EPT, SW], I32)
        scat = sb("scat", [EPP, 2, SC * RW], I32)
        tmpl = sb("tmpl", [P, U * RW], I32)
        tmpls = sb("tmpls", [P, U * SW], I32)
        rec = sb("rec", [P, BODY * RW], I32)
        lane = sb("lane", [P, P])
        ident = sb("ident", [P, P])
        ones = sb("ones", [P, P])
        tri = sb("tri", [P, P])
        tcol = sb("tcol", [P, TB])
        zero = sb("zero", [P, 1])
        epsc = sb("epsc", [P, 1])
        warm = sb("warm", [P, 1])
        cnt = sb("cnt", [P, 2, P])
        blks = sb("blks", [P, 8, 64])
        blki = sb("blki", [P, 64], I32)
        tbf = sb("tbf", [P, 4, TB])
        tbi = sb("tbi", [P, 3, TB], I32)
        tbrow = sb("tbrow", [1, 3, TILES], I32)
        node0 = sb("node0", [P, TILES])
        local = sb("local", [P, 2, U])
        flag = sb("flag", [P, 2])
        flagi = sb("flagi", [P, 1], I32)
        tj = sb("tj", [P, 64])
        wgate = sb("wgate", [P, KC, R])
        wl1 = sb("wl1", [P, KC, D])
        late_w = recs[:, :, :].rearrange("p t w -> p (t w)")[:, 0:4 * KC * D].bitcast(F32)
        wpg = late_w[:, 0:2 * KC * D].rearrange("p (c n) -> p c n", c=KC)
        wab = late_w[:, 2 * KC * D:4 * KC * D].rearrange("p (l c n) -> p l c n", l=2, c=KC)
        weh, wel = sb("weh", [P, 2 * D], R32), sb("wel", [P, 2 * D], R32)
        w2h, w2l = sb("w2h", [P, KC, D], R32), sb("w2l", [P, KC, D], R32)
        bpg = sb("bpg", [P, 2 * D])
        b2w = sb("b2w", [64, D])
        b2h = sb("b2h", [64, D], R32)
        ones_r = sb("ones_r", [64, P], R32)
        rows, o = {}, U * P + BODY * DE
        for name in ("b_l1", "gamma", "beta", "b_a", "g_a", "be_a", "b_b", "g_b", "be_b"):
            k = len(rows)
            rows[name] = early[:, o + k * D:o + (k + 1) * D]
        o += 9 * D
        gate = sb("gate", [P, 2, R])
        xs = sb("xs", [P, 2, D])
        xT = sb("xT", [P, 2, KC, P])
        st = sb("st", [P, 2, 2 * D])
        stats = early[:, o:o + NB * 6].rearrange("p (b w) -> p b w", b=NB)
        mean = sb("mean", [P, NB])
        rstd = sb("rstd", [P, NB])
        lt = sb("lt", [P, 2, NB])
        rdeg = sb("rdeg", [P, NB])
        weighted = early[:, 0:U * P].rearrange("p (s n) -> p s n", s=U)
        onehot = sb("onehot", [P, U, P], R32)
        attr = early[:, U * P:U * P + BODY * DE].rearrange("p (s n) -> p s n", s=BODY)
        ts, sg = (early[:, k * 2 * D:(k + 1) * 2 * D].rearrange("p (s n) -> p s n", s=2) for k in range(2))
        attrT = sb("attrT", [P, 2, P], R32)
        HTh, HTl = sb("HTh", [P, 2, KC, P], R32), sb("HTl", [P, 2, KC, P], R32)
        gs, msg = xs, st[:, :, :].rearrange("p s n -> p (s n)").rearrange("p (s n) -> p s n", s=MS)
        mh, ml = sb("mh", [P, MS, D], R32), sb("ml", [P, MS, D], R32)

        ps = [ctx.enter_context(nc.psum_tensor(f"ps{i}", [P, 512], F32)) for i in range(8)]

        s_ld = {k: sem("ld_" + k) for k in ("edges", "x", "wrel", "wgate", "parts", "late", "last")}
        xpad = sem("xpad")
        consts = sem("consts")
        tmpl_ready, prefilled = sem("tmpl_ready"), sem("prefilled")
        v_sem, a_sem = sem("v_chain"), sem("a_chain")
        raw_used = sem("raw_used")
        counted, based = sem("counted"), sem("based")
        slots_ready = [sem(f"slots_ready{k}") for k in range(2)]
        scratch_free = sem("scratch_free")
        v_branch = sem("v_branch")
        listed = sem("listed")
        tb_ready, tb_stored, tb_back = sem("tb_ready"), sem("tb_stored"), sem("tb_back")
        scat_in = [[sem(f"scat_in{k}{i}") for i in range(2)] for k in range(2)]
        scattered = [[sem(f"scattered{k}{i}") for i in range(2)] for k in range(2)]
        went_on = sem("went_on")
        q = {k: sem("q_" + k) for k in ("xs", "xt", "xtc", "pg", "pr", "gate", "ev", "st0", "st1")}
        acc_clear = sem("acc_clear")
        b2_clear = sem("b2_clear")
        located = sem("located")
        ones_in = sem("ones_in")
        rec_in = [sem(f"rec_in{i}") for i in range(RING)]
        gathered = [sem(f"gathered{i}") for i in range(U)]
        attr_in = [sem(f"attr_in{i}") for i in range(RING)]
        hot = [sem(f"hot{L}") for L in range(5)]
        summed = [sem(f"summed{L}") for L in range(5)]
        done = [sem(f"done{L}") for L in range(5)]
        e = {k: sem("e_" + k) for k in ("at", "atc", "atl", "ht", "relu", "htl", "gp", "gs", "sig", "core", "msg", "mh", "ml")}
        node_sems = ["var", "std", "xs", "sto0", "accok"]
        copy_sems = ["xsc", "sto1"]
        product_sems = ["tp", "tpc", "mm", "st"]
        silu_sems = ["ts", "sg", "ys"]
        n = [{k: sem(f"n{L}_{k}") for k in
              node_sems + copy_sems * (L < 2) + product_sems * (L != 2) + silu_sems * (L > 2)} for L in range(5)]
        x3_added = sem("x3_added")
        xsum, xbeta = sem("xsum"), sem("xbeta")
        x3_in = [sem(f"x3_in{i}") for i in range(2)]
        x3_used, out_ready = sem("x3_used"), sem("out_ready")

        block = ctx.enter_context(nc.Block())

        HALF = {0: 0, 1: 1, 2: 0, 3: 1, 4: 1}
        VIEW = [r_dst.rearrange("(p t) w -> p (t w)", p=P), r_src.rearrange("(p t) w -> p (t w)", p=P)]
        WORDS = [RW, SW]
        PER = [16 * CH if HALF[L] == 0 else 16 for L in range(5)]
        BEFORE = [TURNS * sum(PER[:L]) for L in range(5)]

        def X_(b):
            return X[:, bass.ds(b, 1), :].rearrange("p a w -> p (a w)")

        def X5(b):
            return X[:, bass.ds(b, NI), :]

        def acc5(b):
            return acc[:, bass.ds(b, NI), 0:D]

        def acc_(b, w=D):
            return acc[:, bass.ds(b, 1), 0:w].rearrange("p a w -> p (a w)")

        @block.sync
        def _(sp):
            def load(name, dst_ap, src_ap):
                sp.dma_start(dst_ap, src_ap).then_inc(s_ld[name], 16)

            for L in range(5):
                sp.sem_inc(done[L], BODY)
                for k, v in (("xsc", 2), ("tp", 2), ("tpc", 2), ("mm", 2), ("st", 2), ("ys", 2), ("sto0", 16), ("sto1", 16)):
                    if k in n[L]:
                        sp.sem_inc(n[L][k], v)
            for k, v in (("xt", 2), ("xtc", 2), ("gate", 1), ("ev", 8), ("st0", 16), ("st1", 16)):
                sp.sem_inc(q[k], v)
            for k, v in (("atl", 1), ("gp", 2), ("core", 2), ("msg", 2), ("htl", 2), ("gs", U), ("sig", 2), ("ml", MS)):
                sp.sem_inc(e[k], v)
            sp.sem_inc(x3_used, 2)

            for k, a in enumerate((src, dst, edge_type)):
                load("edges", raw[:, k, :].bitcast(I32), a.rearrange("(p t) -> p t", p=EPP))
            load("edges", raw[0:EPP - 1, 4, :].bitcast(I32), dst[1:E - EPT + 1].rearrange("(p t) -> p t", p=EPP - 1))
            load("edges", raw[EPP - 1:EPP, 4, 0:EPT - 1].bitcast(I32), dst[E - EPT + 1:E].unsqueeze(0))
            load("edges", raw[EPP - 1:EPP, 4, EPT - 1:EPT].bitcast(I32), dst[E - 1:E].unsqueeze(0))
            load("edges", raw[:, 3, :], edge_weight.rearrange("(p t) a -> p (t a)", p=EPP))
            load("x", X[:, 0:FULL, :], x[0:FULL * P, :].rearrange("(b p) f -> p b f", p=P))
            sp.wait_ge(xpad, 1)
            load("x", X[0:TAIL, FULL, :], x[FULL * P:N, :])
            load("wgate", wgate[:, :, :], w_gate.rearrange("(c p) r -> p c r", p=P))
            for c in range(KC):
                load("wrel", wrel[:, c, :].rearrange("p (r o) -> p r o", r=R),
                     w_rel[:, c * P:(c + 1) * P, :].rearrange("r p o -> p r o"))
            sp.wait_ge(tmpl_ready, 2)
            for view, t, w in ((VIEW[0], tmpl, RW), (VIEW[1], tmpls, SW)):
                for k in range(4):
                    n_rep = TILES // U // 4
                    sp.dma_start(view[:, k * n_rep * U * w:(k + 1) * n_rep * U * w].rearrange("p (a w) -> p a w", a=n_rep),
                                 t[:, :].unsqueeze(1).broadcast_to([P, n_rep, U * w])).then_inc(prefilled, 16)
            sp.wait_ge(b2_clear, 1)
            for r in (0, 32):
                load("parts", b2w[r:r + 1, :], b2.rearrange("(a d) -> a d", a=1))
            load("late", wl1[:, :, :], w_l1.rearrange("(c p) o -> p c o", p=P))
            load("late", bpg[:, 0:D], b1.partition_broadcast(P))
            load("late", bpg[:, D:2 * D], bg.partition_broadcast(P))

            def scatter_chunks(k, a, b):
                rw = WORDS[k]
                big = (recd, recs[0:EPP])[k].rearrange("p t w -> p (t w)")
                if a == 0:
                    sp.wait_ge(slots_ready[k], 1)
                    for par in range(2):
                        if k == 0:
                            sp.wait_ge(scattered[1][par], 16 * SC * SPLIT[2])
                        sp.dma_start(scat[:, par, 0:SC * rw], big[:, par * SC * rw:(par + 1) * SC * rw])\
                          .then_inc(scat_in[k][par], 16)
                with sp.Fori(max(a, 1), b) as c:
                    for par in range(2):
                        sp.wait_ge(scattered[k][par], c * (16 * SC))
                        sp.dma_start(scat[:, par, 0:SC * rw], big[:, bass.ds((c * 2 + par) * (SC * rw), SC * rw)])\
                          .then_inc(scat_in[k][par], 16)
                for par in range(2):
                    if b != SPLIT[1]:
                        sp.wait_ge(scattered[k][par], 16 * SC * b)

            def tile_tables():
                sp.wait_ge(tb_ready, 1)
                for k in range(3):
                    sp.dma_start(d_tb[k, :].rearrange("(p j) -> p j", p=P), tbi[:, k, :]).then_inc(tb_stored, 16)
                sp.dma_start(d_tf[0, :].rearrange("(p j) -> p j", p=P), tbf[:, 3, :]).then_inc(tb_stored, 16)
                sp.wait_ge(tb_stored, 64)
                for k in range(3):
                    sp.dma_start(tbrow[:, k, :], d_tb[k:k + 1, 0:TILES]).then_inc(tb_back, 16)
                sp.dma_start(node0[:, :], d_tf[0, 0:TILES].partition_broadcast(P)).then_inc(tb_back, 16)

            first_regs = [sp.alloc_register(f"first{j}") for j in range(BODY)]

            def record_chunks(L, features=False):
                k = HALF[L]
                w = CH * WORDS[k]
                with sp.Fori(0, TURNS) as c:
                    if k == 0:
                        sp.load(first_regs, tbrow[0:1, 2, bass.ds(c * BODY, BODY)])
                    for q_ in range(RING):
                        sp.wait_ge(done[L], c * BODY + (q_ + 1) * CH)
                        if k == 1:
                            sp.dma_start(rec[:, q_ * w:(q_ + 1) * w], VIEW[k][:, bass.ds((c * RING + q_) * w, w)])\
                              .then_inc(rec_in[q_], 16)
                            continue
                        tiles = range(q_ * CH, (q_ + 1) * CH)
                        firsts = [sp.snap(first_regs[j], min_val=0, max_val=SLOTS - P) for j in tiles]
                        for j, first_ in zip(tiles, firsts):
                            sp.dma_start(rec[:, j * RW:(j + 1) * RW], r_dst[bass.ds(first_, P), :])\
                              .then_inc(rec_in[q_], 16)
                        if features:
                            for j, first_ in zip(tiles, firsts):
                                sp.dma_start(attr[:, j, :], edge_attr[bass.ds(first_, P), :])\
                                  .then_inc(attr_in[q_], 16)

            def store_blocks(L, table, buf, ready, credits):
                with sp.Fori(0, NB // 2) as c:
                    for par in range(2):
                        sp.wait_ge(ready, c * 2 + par + (1 + credits))
                        sp.dma_start(table[bass.ds((c * 2 + par) * P, P), :], buf[par])\
                          .then_inc(n[L][f"sto{par}"], 16)

            def store_from_X(L, table, m, ready, credits):
                rows_of = table.rearrange("(b p) f -> p b f", p=P)
                with sp.Fori(0, NB // m) as c:
                    sp.wait_ge(ready, c * m + (m + credits))
                    sp.dma_start(rows_of[:, bass.ds(c * m, m), :], X[:, bass.ds(c * m, m), :]).then_inc(n[L]["sto0"], 16)

            sp.wait_ge(prefilled, 16 * 8)
            scatter_chunks(1, 0, SPLIT[1])
            tile_tables()
            sp.wait_ge(tb_back, 64)
            in_order = sp.value_load(flagi[0:1, 0:1], min_val=0, max_val=1)
            with sp.If(in_order == 1):
                sp.dma_start(r_dst[0:E, :].rearrange("(p t) w -> p (t w)", p=EPP), recd.rearrange("p t w -> p (t w)"))\
                  .then_inc(listed, 16)
            with sp.Else():
                sp.sem_inc(listed, 16)
            scatter_chunks(1, SPLIT[1], SPLIT[2])
            sp.wait_ge(listed, 16)
            with sp.If(in_order == 0):
                scatter_chunks(0, 0, SCHUNKS // 2)
            for h in range(2):
                for k, w in enumerate((w1, wg)):
                    load("parts", st[h * DE:(h + 1) * DE, 0, k * D:(k + 1) * D], w[D:D + DE, :])
            load("parts", st[:, 1, :].rearrange("p (c o) -> p c o", c=KC), w2.rearrange("(c p) o -> p c o", p=P))
            for name, a in (("b_l1", b_l1), ("gamma", gamma), ("beta", beta), ("b_a", b_a), ("g_a", g_a),
                            ("be_a", be_a), ("b_b", b_b), ("g_b", g_b), ("be_b", be_b)):
                load("late", rows[name][:, :], a.partition_broadcast(P))
            record_chunks(0)
            scatter_chunks(1, SPLIT[2], SPLIT[4])
            for a, b in ((wab[:, 0], w_a), (wab[:, 1], w_b), (wpg[:, :, 0:D], w1[0:D, :]), (wpg[:, :, D:2 * D], wg[0:D, :])):
                load("last", a, b.rearrange("(c p) o -> p c o", p=P))
            record_chunks(1)
            store_blocks(1, t_pg, [st[:, par, :] for par in range(2)], n[1]["st"], 2)
            with sp.If(in_order == 1):
                record_chunks(2, features=True)
            with sp.Else():
                record_chunks(2)
            store_from_X(2, t_x3, NI, n[2]["xs"], 0)
            record_chunks(3)
            store_from_X(3, t_y1, NI, n[3]["ys"], 2)
            record_chunks(4)
            sp.wait_ge(n[4]["mm"], NB + 2)
            with sp.Fori(0, NB // 2) as c:
                for par in range(2):
                    sp.wait_ge(x3_used, c * 2 + par + 1)
                    sp.dma_start(xs[:, par, :], t_x3[bass.ds((c * 2 + par) * P, P), :]).then_inc(x3_in[par], 16)
            rows_of = out[0:FULL * P, :].rearrange("(b p) f -> p b f", p=P)
            with sp.Fori(0, FULL // NI) as c:
                sp.wait_ge(out_ready, c * NI + NI)
                sp.dma_start(rows_of[:, bass.ds(c * NI, NI), :], X[:, bass.ds(c * NI, NI), :]).then_inc(n[4]["sto0"], 16)
            sp.wait_ge(out_ready, USED)
            o = FULL // NI * NI
            sp.dma_start(rows_of[:, o:FULL, :], X[:, o:FULL, :]).then_inc(n[4]["sto0"], 16)
            sp.dma_start(out[FULL * P:N, :], X[0:TAIL, FULL, :]).then_inc(n[4]["sto0"], 16)
            sp.wait_ge(n[4]["sto0"], 16 * (FULL // NI + 2) + 16)

        @block.gpsimd
        def _(pool):
            pool.memset(X[:, FULL:NB, :], 0.0).then_inc(xpad, 1)
            pool.memset(ones[:, :], 1.0).then_inc(consts, 1)
            pool.memset(ident[:, :], 0.0).then_inc(consts, 1)
            pool.memset(zero[:, :], 0.0).then_inc(consts, 1)
            pool.memset(cnt[:, :, :], 0.0).then_inc(consts, 1)
            pool.memset(epsc[:, :], EPS).then_inc(consts, 1)
            pool.iota(lane[:, :], [[1, P]], base=0, channel_multiplier=0,
                      allow_small_or_imprecise_dtypes=True).then_inc(consts, 1)
            pool.iota(tcol[:, :], [[1, TB]], base=0, channel_multiplier=TB,
                      allow_small_or_imprecise_dtypes=True).then_inc(consts, 1)
            pool.iota(recd[:, :, 4], [[1, EPT]], base=0, channel_multiplier=EPT).then_inc(consts, 1)
            pool.memset(recd[:, :, RW - 1], 0).then_inc(consts, 1)
            pool.memset(tmpl[:, :], 0).then_inc(consts, 1)
            pool.memset(tmpls[:, :], 0).then_inc(consts, 1)
            pool.memset(b2w[:, :], 0.0).then_inc(b2_clear, 1)
            pool.memset(ones_r[:, :].bitcast(F32), 1.0).then_inc(consts, 1)
            pool.wait_ge(consts, 12)
            pool.affine_select(out=ident[:, :], in_=ident[:, :], compare_op=ALU.not_equal, fill=1.0,
                               base=0, pattern=[[-1, P]], channel_multiplier=1).then_inc(consts, 1)
            pool.affine_select(out=tri[:, :], in_=ones[:, :], compare_op=ALU.is_gt, fill=0.0,
                               base=0, pattern=[[1, P]], channel_multiplier=-1).then_inc(consts, 1)
            pool.memset(tmpl[:, :].bitcast(F32).rearrange("p (t w) -> p t w", w=RW)[:, :, 2], -1.0).then_inc(tmpl_ready, 1)
            pool.memset(tmpls[:, :].bitcast(F32).rearrange("p (t w) -> p t w", w=SW)[:, :, 1], -1.0).then_inc(tmpl_ready, 1)

            def message_low(c, jj):
                T, m = c * BODY + jj, jj % MS
                pool.wait_ge(e["mh"], T + 1)
                pool.wait_ge(done[2], T + 1 + BODY - MS)
                nc.gpsimd.tensor_tensor(ml[:, m, :], msg[:, m, :], mh[:, m, :].bitcast(F32), ALU.subtract)\
                    .then_inc(e["ml"], 1)

            def scatter(k, a, b):
                rw = WORDS[k]
                with pool.Fori(a, b) as c:
                    for par in range(2):
                        pool.wait_ge(scat_in[k][par], c * 16 + 16)
                        pool.sem_inc(went_on, 1)
                        for j in range(SC):
                            r = scat[:, par, j * rw:(j + 1) * rw]
                            pool.indirect_dma_start(out=(r_dst, r_src)[k], in_=r, in_offset=None,
                                                    out_offset=bass.IndirectOffsetOnAxis(ap=r[:, rw - 1:rw], axis=0))\
                                .then_inc(scattered[k][par], 16)

            def gather(L, table, column, width, features=False):
                rw = WORDS[HALF[L]]

                def turn(c, first=False):
                    for j in range(BODY):
                        q_, s, r = j // CH, j % U, rec[:, j * rw:(j + 1) * rw]
                        if j % CH == 0:
                            pool.wait_ge(rec_in[q_], c * PER[L] + (BEFORE[L] + PER[L]))
                            pool.sem_inc(went_on, 1)
                            for t in range(j, j + CH) if features else ():
                                pool.indirect_dma_start(
                                    out=attr[:, t, :], out_offset=None, in_=edge_attr,
                                    in_offset=bass.IndirectOffsetOnAxis(ap=rec[:, t * RW + 4:t * RW + 5], axis=0))\
                                    .then_inc(attr_in[q_], 16)
                        if L == 2:
                            pool.wait_ge(e["gs"], c * BODY + j + 1)
                        else:
                            pool.wait_ge(done[L], c * BODY + j + 1 + U)
                        pool.sem_inc(went_on, 1)
                        pool.indirect_dma_start(out=G[:, s, 0:width], out_offset=None, in_=table,
                                                in_offset=bass.IndirectOffsetOnAxis(ap=r[:, column:column + 1], axis=0))\
                            .then_inc(gathered[s], 16)
                        if L == 2 and not (first and j < LOW_LAG):
                            message_low(c, j - LOW_LAG)

                if L == 2:
                    turn(0, first=True)
                with pool.Fori(int(L == 2), TURNS) as c:
                    turn(c)
                for j in range(BODY - LOW_LAG, BODY if L == 2 else 0):
                    message_low(TURNS - 1, j)

            def clear(L):
                pool.wait_ge(n[L - 1]["accok"], 1)
                pool.memset(accf, 0.0).then_inc(acc_clear, 1)

            pool.wait_ge(prefilled, 16 * 8)
            scatter(1, 0, SPLIT[2])
            pool.wait_ge(tb_ready, 1)
            in_order = pool.value_load(flagi[0:1, 0:1], min_val=0, max_val=1)
            with pool.If(in_order == 0):
                scatter(0, 0, SCHUNKS // 2)
            pool.wait_ge(scratch_free, 1)
            pool.wait_ge(q["ev"], NB * R + 8)
            pool.memset(accf, 0.0).then_inc(acc_clear, 1)

            def stored(L):
                for k in ("sto0", "sto1") if L < 2 else ("sto0",):
                    pool.wait_ge(n[L][k], 16 * (NB // (2 if L < 2 else NI)) + 16)

            for par in range(2):
                pool.wait_ge(q[f"st{par}"], 16 * NB + 16)
            gather(0, t_rel, 0, D)
            scatter(1, SPLIT[2], SPLIT[3])
            clear(1)
            pool.memset(G[:, :, D:D + 1], 1.0).then_inc(ones_in, 1)
            scatter(1, SPLIT[3], SPLIT[4])
            stored(0)
            gather(1, t_h, 0, D)
            clear(2)
            stored(1)
            with pool.If(in_order == 1):
                gather(2, t_pg, 1, 2 * D)
            with pool.Else():
                gather(2, t_pg, 1, 2 * D, features=True)
            with pool.Fori(0, NB // NI) as c:
                pool.wait_ge(xsum, c + 1)
                nc.gpsimd.tensor_tensor(X5(c * NI), X5(c * NI),
                                        rows["beta"][:, :].unsqueeze(1).broadcast_to([P, NI, D]), ALU.add)\
                    .then_inc(xbeta, 1)
            clear(3)
            stored(2)
            gather(3, t_x3, 0, D)
            clear(4)
            stored(3)
            gather(4, t_y1, 0, D)
            with pool.Fori(0, NB // 2) as c:
                for par in range(2):
                    T = c * 2 + par
                    pool.wait_ge(n[4]["ys"], T + 3)
                    pool.wait_ge(x3_in[par], c * 16 + 16)
                    nc.gpsimd.tensor_tensor(X_(T), X_(T), xs[:, par, :], ALU.add).then_inc(x3_added, 1)
                    pool.wait_ge(x3_added, T + 1)
                    pool.sem_inc(x3_used, 1)

        @block.vector
        def _(dve):
            ch = Chain(dve, v_sem)
            V = nc.vector

            dve.wait_ge(s_ld["edges"], 16 * 7)
            dve.wait_ge(consts, 14)
            ri = [raw[:, k, :].bitcast(I32) for k in range(5)]
            sc = ind.bitcast(I32)
            V.scalar_tensor_tensor(out=recd[:, :, 0], in0=ri[0], scalar=float(R), in1=ri[2],
                                   op0=ALU.mult, op1=ALU.add)
            V.tensor_copy(recd[:, :, 1], ri[0])
            V.tensor_copy(recd[:, :, 3].bitcast(F32), raw[:, 3, :])
            V.tensor_copy(recs[0:EPP, :, 0], ri[1])
            V.tensor_copy(recd[:, :, 2].bitcast(F32), ri[1])
            ch.step(V.tensor_tensor(run, ri[1], ri[4], ALU.is_gt))
            ch.wait()
            ch.step(V.tensor_reduce(cnt[0:EPP, 0, USED:USED + 1], run, mybir.AxisListType.X, ALU.add))
            ch.step(V.tensor_scalar(sc, ri[0], P - 1, None, ALU.bitwise_and))
            ch.wait()
            ch.step(V.tensor_copy(recs[0:EPP, :, 1].bitcast(F32), sc))
            ch.wait()
            for key, r in ((1, ri[1]), (0, ri[0])):
                ch.step(V.tensor_scalar(sc, r, 7, None, ALU.arith_shift_right))
                ch.wait()
                ch.step(V.tensor_copy(blk["dst" if key else "src"], sc))
                ch.wait()
            V.memset(tj[:, :], 0.0).then_inc(raw_used, 1)

            total, before, nt, end, first, base, shift = (blks[:, i, :] for i in range(7))

            def count(k, key):
                def in_block(d, scratch):
                    ch.step(V.tensor_scalar(scratch, blk[key], lane[0:EPP, bass.ds(d, 1)], None, ALU.is_equal, ALU.add,
                                            accum_out=cnt[0:EPP, k, bass.ds(d, 1)]))

                ch.wait()
                in_block(0, ind)
                with dve.Fori(0, USED // 2) as c:
                    ch.enter(c, 2)
                    for p_ in range(2):
                        ch.wait_but_one()
                        in_block(c * 2 + (p_ + 1), (run, ind)[p_])
                    ch.leave(USED // 2)
                ch.wait()
                dve.sem_inc(counted, 1)
                dve.wait_ge(based, 2 - k)
                ch.step(V.tensor_copy(total[:, 0:USED + 1], ps[7][:, (2 * k + 1) * P:(2 * k + 1) * P + USED + 1]))
                ch.step(V.tensor_copy(before[:, 0:USED], ps[7][:, 2 * k * P:2 * k * P + USED]))
                ch.wait()
                u = slice(0, USED)
                ch.step(V.tensor_scalar(blki[:, u], total[:, u], float(P - 1), None, ALU.add))
                ch.wait()
                ch.step(V.tensor_scalar(blki[:, u], blki[:, u], 7, None, ALU.arith_shift_right))
                ch.wait()
                ch.step(V.tensor_copy(nt[:, u], blki[:, u]))
                ch.wait()
                ch.step(V.tensor_tensor_scan(end[:, u], ones[:, u], nt[:, u], 0.0, ALU.mult, ALU.add))
                ch.wait()
                ch.step(V.tensor_tensor(first[:, u], end[:, u], nt[:, u], ALU.subtract))
                ch.wait()
                ch.step(V.scalar_tensor_tensor(out=base[:, u], in0=first[:, u], scalar=float(P), in1=before[:, u],
                                               op0=ALU.mult, op1=ALU.add))
                ch.wait()
                ch.step(V.tensor_scalar(blks[:, 6 + k, u], base[:, u], -1.0, None, ALU.add))
                ch.wait()
                m = slice(0, USED - 1)
                for j in range(TB):
                    ch.step(V.tensor_scalar(tj[:, m], end[:, m], tcol[:, j:j + 1], None, ALU.is_le, ALU.add,
                                            accum_out=tbf[:, k, j:j + 1]))
                    ch.wait()
                if k == 0:
                    ch.step(V.tensor_scalar(flag[:, 0:1], total[:, USED:USED + 1], 0.0, None, ALU.is_equal))
                    ch.step(V.scalar_tensor_tensor(out=base[:, u], in0=nt[:, u], scalar=-float(P), in1=total[:, u],
                                                   op0=ALU.mult, op1=ALU.add))
                    ch.wait()
                    ch.step(V.tensor_scalar(base[:, u], base[:, u], flag[:, 0:1], None, ALU.mult))
                    ch.step(V.tensor_copy(flagi[:, :], flag[:, 0:1]))
                    ch.step(V.tensor_scalar(tbf[:, 3, :], tbf[:, 0, :], float(P), None, ALU.mult))
                    ch.wait()
                    for j in range(TB):
                        ch.step(V.tensor_scalar(tj[:, m], end[:, m], tcol[:, j:j + 1], None, ALU.is_le))
                        ch.wait()
                        ch.step(V.tensor_tensor(tj[:, m], tj[:, m], base[:, m], ALU.mult))
                        ch.wait()
                        ch.step(V.tensor_reduce(tbf[:, 2, j:j + 1], tj[:, m], mybir.AxisListType.X, ALU.add))
                        ch.wait()
                    ch.step(V.scalar_tensor_tensor(out=tbf[:, 2, :], in0=tcol[:, :], scalar=float(P), in1=tbf[:, 2, :],
                                                   op0=ALU.mult, op1=ALU.add))

            def find_slots(k, key, ch):
                def in_block(d, to):
                    ch.step(V.tensor_scalar(to, blk[key], lane[0:EPP, bass.ds(d, 1)], None, ALU.is_equal))

                def count_up(d, of, to):
                    ch.step(V.tensor_tensor_scan(to, of, zero[0:EPP, 0:1].to_broadcast([EPP, EPT]),
                                                 blks[0:EPP, 6 + k, bass.ds(d, 1)], ALU.add, ALU.add))

                def keep(of, numbers):
                    dve.sem_inc(went_on, 1)
                    ch.step(V.copy_predicated(slot, of.bitcast(I32), numbers))

                if k == 0:
                    with dve.Fori(0, USED) as d:
                        ch.enter(d, 3)
                        ch.wait()
                        in_block(d, ind)
                        ch.wait()
                        count_up(d, ind, run)
                        ch.wait()
                        keep(ind, run)
                        ch.leave(USED)
                else:
                    inds = (ind, st[0:EPP, :, :].rearrange("p s n -> p (s n)")[:, 0:EPT])
                    runs = (run, node0[0:EPP, 0:EPT])
                    in_block(0, inds[0])
                    with dve.Fori(0, USED // 2) as c:
                        ch.enter(c, 6)
                        for p_ in range(2):
                            if p_ == 0:
                                ch.wait()
                            else:
                                ch.wait_but_one()
                            count_up(c * 2 + p_, inds[p_], runs[p_])
                            ch.wait_but_one()
                            in_block(c * 2 + (p_ + 1), inds[1 - p_])
                            ch.wait_but_one()
                            keep(inds[p_], runs[p_])
                        ch.leave(USED // 2)
                    ch.wait()
                    count_up(USED - 1, inds[0], runs[0])
                    ch.wait()
                    keep(inds[0], runs[0])
                ch.wait()
                if k == 0:
                    ch.step(V.tensor_copy(recd[:, :, RW - 1], slot))
                else:
                    si, hi = ind.bitcast(I32), run.bitcast(I32)
                    ch.step(V.tensor_copy(si, slot))
                    ch.wait()
                    ch.step(V.tensor_scalar(hi, si, 7, None, ALU.arith_shift_right))
                    ch.step(V.tensor_scalar(slot.bitcast(I32), si, P - 1, None, ALU.bitwise_and))
                    ch.wait()
                    ch.step(V.scalar_tensor_tensor(out=recs[0:EPP, :, SW - 1], in0=slot.bitcast(I32), scalar=float(TILES),
                                                   in1=hi, op0=ALU.mult, op1=ALU.add))
                ch.wait()
                dve.sem_inc(slots_ready[k], 1)

            count(1, "src")
            ch.wait()
            find_slots(1, "src", ch)
            count(0, "dst")
            ch.wait()
            ch.step(V.tensor_copy(tbi[:, :, :], tbf[:, 0:3, :]))
            ch.wait()
            dve.sem_inc(tb_ready, 1)
            in_order = dve.value_load(flagi[0:1, 0:1], min_val=0, max_val=1)
            with dve.If(in_order == 0):
                find_slots(0, "dst", Chain(dve, v_branch))
            dve.sem_inc(scratch_free, 1)

            dve.wait_ge(s_ld["parts"], 16 * 7)

            def part(raw_ap, high, low):
                ch.step(V.tensor_copy(high, raw_ap))
                ch.wait()
                ch.step(V.tensor_tensor(low, raw_ap, high.bitcast(F32), ALU.subtract))

            part(st[:, 0, :], weh[:, :], wel[:, :])
            part(st[:, 1, :].rearrange("p (c o) -> p c o", c=KC), w2h[:, :, :], w2l[:, :, :])
            ch.wait()
            b2t = st[0:64, 0, 0:D]
            ch.step(V.memset(b2h[:, :].bitcast(F32), 0.0))
            ch.wait()
            ch.step(V.tensor_copy(b2h[:, :], b2w[:, :]))
            ch.wait()
            ch.step(V.tensor_tensor(b2t, b2w[:, :], b2h[:, :].bitcast(F32), ALU.subtract))
            ch.wait()
            ch.step(V.tensor_copy(b2h[32:33, :], b2t[32:33, :]))
            ch.wait()

            blk_regs = [dve.alloc_register(f"blk{j}") for j in range(BODY)]

            def load_blocks(k, c):
                dve.load(blk_regs, tbrow[0:1, k, bass.ds(c * BODY, BODY)])

            def make_hot(L, T, j, c):
                rw = WORDS[HALF[L]]
                par, s = j // U, j % U
                if s == 0:
                    for q_ in range(par * U // CH, (par + 1) * U // CH):
                        dve.wait_ge(rec_in[q_], c * PER[L] + (BEFORE[L] + PER[L]))
                    if HALF[L] == 0:
                        dst_of = rec[:, par * U * RW:(par + 1) * U * RW].bitcast(F32).rearrange("p (t w) -> p t w", w=RW)[:, :, 2]
                        V.tensor_tensor(local[:, par, :], dst_of, node0[:, bass.ds(c * BODY + par * U, U)], ALU.subtract)\
                            .then_inc(located, 1)
                        turns = TURNS * 2 * (L // 2)
                        dve.wait_ge(located, c * 2 + (par + 1 + turns))
                r = rec[:, j * rw:(j + 1) * rw].bitcast(F32)
                node = local[:, par, s:s + 1] if HALF[L] == 0 else r[:, 1:2]
                if L == 0:
                    V.tensor_scalar(weighted[:, s, :], lane[:, :], node, r[:, 3:4], ALU.is_equal, ALU.mult)\
                        .then_inc(hot[L], 1)
                else:
                    V.tensor_scalar(onehot[:, s, :], lane[:, :], node, None, ALU.is_equal).then_inc(hot[L], 1)

            def add_tile(L, T, j, width, bank):
                b = dve.snap(blk_regs[j], min_val=0, max_val=USED - 1)
                dve.wait_ge(summed[L], T + 1)
                dve.wait_ge(done[L], T + BODY)
                a = acc_(b, width)
                V.tensor_tensor(a, a, bank[:, 0:width], ALU.add).then_inc(done[L], 1)

            def edge_adds(L, width):
                dve.wait_ge(acc_clear, L + 1)
                dve.wait_ge(tb_back, 64)
                LAG = 3
                with dve.Fori(0, TURNS) as c:
                    load_blocks(HALF[L], c)
                    for j in range(BODY + LAG):
                        if j < BODY:
                            make_hot(L, c * BODY + j, j, c)
                        if j >= LAG:
                            add_tile(L, c * BODY + j - LAG, j - LAG, width, ps[(j - LAG) % 4])

            def attr_low(c, jj):
                T, o = c * BODY + jj, jj % 2
                dve.wait_ge(e["atc"], T + 1)
                V.tensor_tensor(attrT[DE:P, o, :], ps[0][0:DE, 0:P], attrT[0:DE, o, :].bitcast(F32), ALU.subtract)\
                    .then_inc(e["atl"], 1)

            def hidden_low(c, jj):
                T, o = c * BODY + jj, jj % 2
                dve.wait_ge(e["relu"], T + 1)
                V.scalar_tensor_tensor(out=HTl[:, o, :, :].rearrange("p c n -> p (c n)"), in0=ps[1 + o][:, 0:D],
                                       scalar=0.0, in1=HTh[:, o, :, :].rearrange("p c n -> p (c n)").bitcast(F32),
                                       op0=ALU.max, op1=ALU.subtract).then_inc(e["htl"], 1)

            def gate_sum(c, jj):
                T, o = c * BODY + jj, jj % 2
                dve.wait_ge(e["gp"], T + 3)
                dve.wait_ge(e["sig"], T + 1)
                V.tensor_tensor(gs[:, o, :], ps[3 + o][:, 0:D], G[:, jj % U, D:2 * D], ALU.add).then_inc(e["gs"], 1)

            def message(c, jj):
                T, o = c * BODY + jj, jj % 2
                dve.wait_ge(e["sig"], T + 3)
                dve.wait_ge(e["core"], T + 3)
                dve.wait_ge(e["ml"], T + 1)
                V.tensor_tensor(msg[:, jj % MS, :], ps[5 + o][:, 0:D], sg[:, o, :], ALU.mult).then_inc(e["msg"], 1)

            def edge2_turn(c, first=False, last=False):
                if first:
                    load_blocks(0, c)
                for j in range(BODY):
                    if j == SUM_LAG and not first:
                        load_blocks(0, c)
                    make_hot(2, c * BODY + j, j, c)
                    if not (last and j == BODY - 1):
                        attr_low(c, j + 1)
                    hidden_low(c, j)
                    gate_sum(c, j)
                    if not first or j >= 1:
                        message(c, j - 1)
                    if not first or j >= SUM_LAG:
                        add_tile(2, c * BODY + (j - SUM_LAG), (j - SUM_LAG) % BODY, D, ps[7])

            def edge2():
                dve.wait_ge(acc_clear, 3)
                attr_low(0, 0)
                edge2_turn(0, first=True)
                with dve.Fori(1, TURNS - 1) as c:
                    edge2_turn(c)
                edge2_turn(TURNS - 1, last=True)
                message(TURNS - 1, BODY - 1)
                for j in range(BODY - SUM_LAG, BODY):
                    add_tile(2, (TURNS - 1) * BODY + j, j, D, ps[7])

            def finish_stats(L, which):
                ch.wait()
                s = stats[:, :, :]
                ch.step(V.tensor_tensor(lt[:, 0, :], s[:, :, 1], s[:, :, 4], ALU.add))
                ch.step(V.tensor_tensor(lt[:, 1, :], s[:, :, 1], s[:, :, 4], ALU.subtract))
                ch.step(V.tensor_tensor(rstd[:, :], s[:, :, 2], s[:, :, 5], ALU.add))
                ch.wait()
                ch.step(V.tensor_scalar(mean[:, :], lt[:, 0, :], 0.5, None, ALU.mult))
                ch.step(V.tensor_tensor(lt[:, 1, :], lt[:, 1, :], lt[:, 1, :], ALU.mult))
                ch.step(V.tensor_scalar(rstd[:, :], rstd[:, :], 1.0 / D, None, ALU.mult))
                ch.wait()
                ch.step(V.scalar_tensor_tensor(out=lt[:, 0, :], in0=lt[:, 1, :], scalar=0.25, in1=rstd[:, :],
                                               op0=ALU.mult, op1=ALU.add))
                ch.wait()
                dve.sem_inc(n[L]["var"], 1)
                dve.wait_ge(n[L]["std"], which + 1)
                ch.step(V.reciprocal(rstd[:, :], lt[:, 1, :]))
                ch.wait()

            def stat(b, of):
                V_out = stats[:, bass.ds(b, 1), :].rearrange("p a w -> p (a w)")
                ch.step(V.bn_stats(V_out, of))

            def normed(dst_ap, of, b):
                return V.tensor_scalar(dst_ap, of, mean[:, bass.ds(b, 1)], rstd[:, bass.ds(b, 1)],
                                       ALU.subtract, ALU.mult)

            def residual(L, relu):
                with dve.Fori(0, NB // NI) as c:
                    ch.enter(c, 1 + NI)
                    if relu:
                        ch.step(V.scalar_tensor_tensor(out=X5(c * NI), in0=acc5(c * NI), scalar=0.0, in1=X5(c * NI),
                                                       op0=ALU.max, op1=ALU.add))
                    else:
                        ch.step(V.tensor_tensor(X5(c * NI), acc5(c * NI), X5(c * NI), ALU.add))
                    ch.wait()
                    for i in range(NI):
                        stat(c * NI + i, X_(c * NI + i))
                    ch.leave(NB // NI)
                ch.wait()

            def two_deep(before, after, per):
                before(0)
                with dve.Fori(0, NB // 2 - 1) as c:
                    ch.enter(c, per)
                    before(c + 1)
                    after(c)
                    ch.leave(NB // 2 - 1)
                after(NB // 2 - 1)

            def rolling(before, after, per):
                for par in range(2):
                    before(par, par)
                with dve.Fori(0, NB // 2 - 1) as c:
                    ch.enter(c, per)
                    for par in range(2):
                        before(c * 2 + (2 + par), par)
                        after(c * 2 + par, par)
                    ch.leave(NB // 2 - 1)
                for par in range(2):
                    after(NB - 2 + par, par)

            def normalise_and_bias(L, width, bias):
                S = n[L]

                def before(T, par):
                    dve.wait_ge(S["xsc"], T + 1)
                    dve.wait_ge(S["tp"], T + 1)
                    normed(xs[:, par, :], X_(T), T).then_inc(S["xs"], 1)

                def after(T, par):
                    dve.wait_ge(S["mm"], T + 3)
                    dve.wait_ge(S[f"sto{par}"], T * 8 + (16 - 8 * par))
                    V.tensor_tensor(st[:, par, 0:width], ps[par][:, 0:width], bias, ALU.add).then_inc(S["st"], 1)

                rolling(before, after, 0)

            edge_adds(0, D)
            dve.wait_ge(done[0], TILES + BODY)
            dve.wait_ge(s_ld["x"], 32)
            dve.wait_ge(s_ld["late"], 16 * LATE)
            residual(0, True)
            finish_stats(0, 0)
            dve.sem_inc(n[0]["accok"], 1)
            normalise_and_bias(0, D, rows["b_l1"][:, :])

            edge_adds(1, AW)
            dve.wait_ge(done[1], TILES + BODY)
            dve.wait_ge(n[0]["xsc"], NB + 2)
            residual(1, False)
            ch.step(V.tensor_scalar(rdeg[:, :], acc[:, :, D], 1.0, None, ALU.max))
            ch.wait()
            ch.step(V.reciprocal(rdeg[:, :], rdeg[:, :]))
            finish_stats(1, 0)
            dve.sem_inc(n[1]["accok"], 1)
            normalise_and_bias(1, 2 * D, bpg[:, :])

            edge2()
            dve.wait_ge(done[2], TILES + BODY)
            dve.wait_ge(n[1]["xsc"], NB + 2)
            with dve.Fori(0, NB // NI) as c:
                ch.enter(c, 1 + NI)
                ch.step(V.tensor_tensor(acc5(c * NI), acc5(c * NI), X5(c * NI), ALU.add))
                ch.wait()
                dve.sem_inc(xsum, 1)
                for i in range(NI):
                    stat(c * NI + i, acc_(c * NI + i))
                ch.leave(NB // NI)
            finish_stats(2, 0)
            with dve.Fori(0, NB // NI) as c:
                ch.enter(c, 3 * NI)
                for i in range(NI):
                    b = c * NI + i
                    ch.step(V.scalar_tensor_tensor(out=acc_(b), in0=acc_(b), scalar=mean[:, bass.ds(b, 1)],
                                                   in1=rows["gamma"][:, :], op0=ALU.subtract, op1=ALU.mult))
                dve.wait_ge(xbeta, c + 1)
                for i in range(NI):
                    b = c * NI + i
                    ch.wait_for(i + 1)
                    ch.step(V.scalar_tensor_tensor(out=acc_(b), in0=acc_(b), scalar=rstd[:, bass.ds(b, 1)],
                                                   in1=X_(b), op0=ALU.mult, op1=ALU.add))
                for i in range(NI):
                    ch.wait_for(NI + i + 1)
                    stat(c * NI + i, acc_(c * NI + i))
                ch.leave(NB // NI)
            finish_stats(2, 1)
            with dve.Fori(0, NB // NI) as c:
                for i in range(NI):
                    normed(X_(c * NI + i), acc_(c * NI + i), c * NI + i).then_inc(n[2]["xs"], 1)
            dve.wait_ge(n[2]["xs"], NB)
            dve.sem_inc(n[2]["accok"], 1)

            for L, bias, g, be in ((3, "b_a", "g_a", "be_a"), (4, "b_b", "g_b", "be_b")):
                S = n[L]
                edge_adds(L, D)
                dve.wait_ge(done[L], TILES + BODY)
                def before(T, par):
                    dve.wait_ge(S["tp"], T + 1)
                    V.scalar_tensor_tensor(out=xs[:, par, :], in0=acc_(T), scalar=rdeg[:, bass.ds(T, 1)],
                                           in1=X_(T), op0=ALU.mult, op1=ALU.add).then_inc(S["xs"], 1)

                def after(T, par):
                    dve.wait_ge(S["mm"], T + 3)
                    dve.wait_ge(S["xs"], T + 1)
                    V.tensor_tensor(acc_(T), ps[par][:, 0:D], rows[bias][:, :], ALU.add).then_inc(S["st"], 1)
                    if par == 1:
                        for b in (T - 1, T):
                            dve.wait_ge(S["st"], b + 3)
                            stat(b, acc_(b))

                rolling(before, after, 2)
                finish_stats(L, 0)

                def before(c):
                    m = ch.n
                    for par in range(2):
                        T = c * 2 + par
                        ch.step(V.scalar_tensor_tensor(out=acc_(T), in0=acc_(T), scalar=mean[:, bass.ds(T, 1)],
                                                       in1=rows[g][:, :], op0=ALU.subtract, op1=ALU.mult))
                    for par in range(2):
                        T = c * 2 + par
                        ch.wait_for(m + par + 1)
                        V.scalar_tensor_tensor(out=acc_(T), in0=acc_(T), scalar=rstd[:, bass.ds(T, 1)],
                                               in1=rows[be][:, :], op0=ALU.mult, op1=ALU.add).then_inc(S["ts"], 1)

                def after(c):
                    for par in range(2):
                        T = c * 2 + par
                        dve.wait_ge(S["sg"], T + 1)
                        V.tensor_tensor(X_(T), acc_(T), sg[:, par, :], ALU.mult).then_inc(S["ys"], 1)

                two_deep(before, after, 2)
                if L == 3:
                    dve.wait_ge(S["ys"], NB + 2)
                    dve.sem_inc(S["accok"], 1)
            with dve.Fori(0, NB // NI) as c:
                ch.enter(c, NI)
                dve.wait_ge(x3_added, c * NI + NI)
                for i in range(NI):
                    stat(c * NI + i, X_(c * NI + i))
                ch.leave(NB // NI)
            finish_stats(4, 1)
            with dve.Fori(0, NB // NI) as c:
                for i in range(NI):
                    normed(X_(c * NI + i), X_(c * NI + i), c * NI + i).then_inc(out_ready, 1)

        @block.scalar
        def _(act):
            A = nc.scalar

            def warm_sigmoid():
                A.activation(warm[:, :], zero[:, :], ACT.Sigmoid).then_inc(went_on, 1)

            def into_X(sem_, value, T, of):
                act.wait_ge(sem_, value)
                act.sem_inc(went_on, 1)
                return A.activation(X_(T), of, ACT.Copy)

            act.wait_ge(s_ld["x"], 32)
            act.wait_ge(raw_used, 1)
            warm_sigmoid()
            trows = t_rel.rearrange("(m r) d -> m (r d)", r=R)

            def copied(T, par):
                act.wait_ge(q["xt"], T + 1)
                act.sem_inc(went_on, 1)
                A.activation(xs[:, par, :], X_(T), ACT.Copy).then_inc(q["xs"], 1)

            def turned(T, par):
                act.wait_ge(q["xt"], T + 3)
                A.activation(xT[:, par, :, :], ps[4 + par][:, 0:D].rearrange("p (c n) -> p c n", c=KC), ACT.Copy)\
                    .then_inc(q["xtc"], 1)

            def gates(T, par):
                act.wait_ge(q["pg"], T + 1)
                A.activation(gate[:, par, :], ps[6][:, 0:R], ACT.Sigmoid).then_inc(q["gate"], 1)

            def relations(c, last_turn=False):
                for par in range(2):
                    T = c * 2 + par
                    ahead = not (last_turn and par == 1)
                    if ahead:
                        turned(T + 1, 1 - par)
                    if not last_turn:
                        copied(T + 2, par)
                    act.wait_ge(q["gate"], T + 2)
                    for g in range(R // 2):
                        h = g // 4
                        if g == R // 4 and ahead:
                            gates(T + 1, 1 - par)
                        act.wait_ge(q["pr"], T * (R // 2) + (g + 1))
                        if g % 4 == 0:
                            act.wait_ge(q[f"st{h}"], T * 16 + 16)
                        for r in range(2):
                            A.activation(stage[:, h, ((g % 4) * 2 + r) * D:((g % 4) * 2 + r + 1) * D],
                                         ps[g % 4][:, r * D:(r + 1) * D], ACT.Copy,
                                         scale=gate[:, par, 2 * g + r:2 * g + r + 1]).then_inc(q["ev"], 1)
                        if g % 4 == 3:
                            act.wait_ge(q["ev"], T * R + (8 * (h + 1) + 8))
                            act.dma_start(trows[bass.ds(T * P, P), h * 8 * D:(h + 1) * 8 * D], stage[:, h, :])\
                               .then_inc(q[f"st{h}"], 16)

            copied(0, 0)
            copied(1, 1)
            turned(0, 0)
            gates(0, 0)
            with act.Fori(0, NB // 2 - 1) as c:
                relations(c)
            relations(NB // 2 - 1, last_turn=True)

            def std(L, which):
                act.wait_ge(n[L]["var"], which + 1)
                A.activation(lt[:, 1, :], lt[:, 0, :], ACT.Sqrt, bias=epsc[:, 0:1]).then_inc(n[L]["std"], 1)

            def transposed(L, T, par):
                S = n[L]
                act.wait_ge(S["tp"], T + 3)
                act.wait_ge(S["mm"], T + 1)
                A.activation(xT[:, par, :, :], ps[6 + par][:, 0:D].rearrange("p (c n) -> p c n", c=KC), ACT.Copy)\
                    .then_inc(S["tpc"], 1)

            def node_plain(L):
                std(L, 0)

                def turn(c, first=False):
                    for par in range(2):
                        T = c * 2 + par
                        into_X(n[L]["xs"], T + 1, T, xs[:, par, :]).then_inc(n[L]["xsc"], 1)
                        transposed(L, T, par)
                        if L == 0 and not (first and par == 0):
                            store(T - 1, 1 - par)

                def store(T, par):
                    act.wait_ge(n[L]["st"], T + 3)
                    act.dma_start(t_h[bass.ds(T * P, P), :], st[:, par, 0:D]).then_inc(n[L][f"sto{par}"], 16)

                turn(0, first=True)
                with act.Fori(1, NB // 2) as c:
                    turn(c)
                if L == 0:
                    store(NB - 1, 1)

            node_plain(0)
            node_plain(1)

            def attr_high(T, jj):
                act.wait_ge(e["at"], T + 1)
                act.wait_ge(e["gp"], T + 1)
                A.activation(attrT[0:DE, jj % 2, :], ps[0][0:DE, 0:P], ACT.Copy).then_inc(e["atc"], 1)

            def message_high(T, jj):
                act.wait_ge(e["msg"], T + 3)
                act.wait_ge(done[2], T + 1 + BODY - MS)
                A.activation(mh[:, jj % MS, :], msg[:, jj % MS, :], ACT.Copy).then_inc(e["mh"], 1)

            def gate_of(T, jj):
                act.wait_ge(e["gs"], T + 1 + U)
                act.wait_ge(e["msg"], T + 1)
                A.activation(sg[:, jj % 2, :], gs[:, jj % 2, :], ACT.Sigmoid).then_inc(e["sig"], 1)

            def act_step(T, j, first=False, last=False):
                if not last:
                    attr_high(T + 1, j + 1)
                act.wait_ge(e["ht"], T + 1)
                act.wait_ge(e["core"], T + 1)
                A.activation(HTh[:, j % 2, :, :], ps[1 + j % 2][:, 0:D].rearrange("p (c n) -> p c n", c=KC), ACT.Relu)\
                    .then_inc(e["relu"], 1)
                if not first or j >= 1:
                    gate_of(T - 1, j - 1)
                if not first or j >= 2:
                    message_high(T - 2, j - 2)

            warm_sigmoid()
            attr_high(0, 0)
            for j in range(BODY):
                act_step(j, j, first=True)
            with act.Fori(1, TURNS - 1) as c:
                for j in range(BODY):
                    act_step(c * BODY + j, j)
            for j in range(BODY):
                act_step((TURNS - 1) * BODY + j, j, last=j == BODY - 1)
            gate_of(TURNS * BODY - 1, BODY - 1)
            for j in (BODY - 2, BODY - 1):
                message_high((TURNS - 1) * BODY + j, j)

            std(2, 0)
            std(2, 1)
            for L in (3, 4):
                S = n[L]
                with act.Fori(0, NB // 2) as c:
                    for par in range(2):
                        transposed(L, c * 2 + par, par)
                std(L, 0)
                warm_sigmoid()
                with act.Fori(0, NB // 2) as c:
                    for par in range(2):
                        T = c * 2 + par
                        act.wait_ge(S["ts"], T + 1)
                        act.wait_ge(S["ys"], T + 1)
                        act.sem_inc(went_on, 1)
                        A.activation(sg[:, par, :], acc_(T), ACT.Sigmoid).then_inc(S["sg"], 1)
            std(4, 1)

        @block.tensor
        def _(pe):
            T_ = nc.tensor

            pe.wait_ge(consts, 14)

            def bases(k):
                pe.wait_ge(counted, 2 - k)
                for h, m in enumerate((tri, ones)):
                    last = T_.matmul(ps[7][:, (2 * k + h) * P:(2 * k + h) * P + USED + 1], m[0:EPP, :],
                                     cnt[0:EPP, k, 0:USED + 1], start=True, stop=True)
                last.then_inc(based, 1)

            bases(1)

            pe.wait_ge(s_ld["wgate"], 16)
            pe.wait_ge(s_ld["wrel"], 32)
            def turned(T, par):
                pe.wait_ge(q["xs"], T + 1)
                pe.wait_ge(q["xtc"], T + 1)
                for k in range(KC):
                    last = T_.transpose(ps[4 + par][:, k * P:(k + 1) * P], xs[:, par, k * P:(k + 1) * P], ident[:, :])
                last.then_inc(q["xt"], 1)

            def gates(T, par):
                pe.wait_ge(q["xtc"], T + 3)
                pe.wait_ge(q["gate"], T + 1)
                for k in range(KC):
                    last = T_.matmul(ps[6][:, 0:R], xT[:, par, k, :], wgate[:, k, :], start=k == 0, stop=k == KC - 1)
                last.then_inc(q["pg"], 1)

            def relations(c, last_turn=False):
                for par in range(2):
                    T = c * 2 + par
                    ahead = not (last_turn and par == 1)
                    if ahead:
                        turned(T + 1, 1 - par)
                    for g in range(R // 2):
                        if g == R // 4 and ahead:
                            gates(T + 1, 1 - par)
                        pe.wait_ge(q["ev"], T * R + (2 * g + 2))
                        for k in range(KC):
                            last = T_.matmul(ps[g % 4][:, :], xT[:, par, k, :], wrel[:, k, g * 2 * D:(g + 1) * 2 * D],
                                             start=k == 0, stop=k == KC - 1)
                        last.then_inc(q["pr"], 1)

            turned(0, 0)
            gates(0, 0)
            with pe.Fori(0, MORE_BLOCKS) as c:
                relations(c)
            bases(0)
            with pe.Fori(MORE_BLOCKS, NB // 2 - 1) as c:
                relations(c)
            relations(NB // 2 - 1, last_turn=True)

            def rows_in(L, c, jj):
                pe.wait_ge(gathered[jj % U], (c * 2 + (jj // U + 1 + 2 * TURNS * L)) * 16)

            def edge_sums(L, width):
                with pe.Fori(0, TURNS) as c:
                    for j in range(BODY):
                        pe.wait_ge(hot[L], c * BODY + j + 1)
                        rows_in(L, c, j)
                        pe.wait_ge(done[L], c * BODY + j + (1 + BODY - 4))
                        rows_of = weighted[:, j % U, :] if L == 0 else onehot[:, j % U, :].bitcast(F32)
                        T_.matmul(ps[j % 4][:, 0:width], rows_of, G[:, j % U, 0:width],
                                  start=True, stop=True).then_inc(summed[L], 1)

            def transposes(L, T, par):
                S = n[L]
                pe.wait_ge(S["xs"], T + 1)
                pe.wait_ge(S["tpc"], T + 1)
                for k in range(KC):
                    last = T_.transpose(ps[6 + par][:, k * P:(k + 1) * P], xs[:, par, k * P:(k + 1) * P], ident[:, :])
                last.then_inc(S["tp"], 1)

            def products(L, weights, width):
                S = n[L]

                def multiply(T, par):
                    pe.wait_ge(S["tpc"], T + 3)
                    pe.wait_ge(S["st"], T + 1)
                    for k in range(KC):
                        last = T_.matmul(ps[par][:, 0:width], xT[:, par, k, :], weights[:, k, :],
                                         start=k == 0, stop=k == KC - 1)
                    last.then_inc(S["mm"], 1)

                transposes(L, 0, 0)
                with pe.Fori(0, NB // 2 - 1) as c:
                    for par in range(2):
                        transposes(L, c * 2 + (1 + par), 1 - par)
                        multiply(c * 2 + par, par)
                transposes(L, NB - 1, 1)
                for par in range(2):
                    multiply(NB - 2 + par, par)

            edge_sums(0, D)
            pe.wait_ge(s_ld["late"], 16 * LATE)
            products(0, wl1, D)
            pe.wait_ge(ones_in, 1)
            edge_sums(1, AW)
            pe.wait_ge(s_ld["last"], 16 * 4)
            products(1, wpg, 2 * D)

            def A(c, jj):
                pe.wait_ge(attr_in[jj // CH % RING], (c + (jj // BODY + 1)) * (16 * CH))
                pe.wait_ge(e["atl"], c * BODY + (jj + 1))
                pe.sem_inc(went_on, 1)
                T_.transpose(ps[0][0:DE, 0:P], attr[:, jj % BODY, :], ident[:, :]).then_inc(e["at"], 1)

            def B(c, jj):
                T, s = c * BODY + jj, jj % U
                rows_in(2, c, jj)
                pe.wait_ge(e["atl"], T + 2)
                pe.wait_ge(e["htl"], T + 1)
                for k in range(KC):
                    o = ps[1 + jj % 2][:, k * P:(k + 1) * P]
                    T_.matmul(o, G[:, s, k * P:(k + 1) * P], ident[:, :], is_transpose=True, start=True, stop=False)
                    T_.matmul(o, weh[:, k * P:(k + 1) * P], attrT[:, jj % 2, :], start=False, stop=False)
                    last = T_.matmul(o, wel[:, k * P:(k + 1) * P], attrT[:, jj % 2, :], start=False, stop=True)
                last.then_inc(e["ht"], 1)
                pe.wait_ge(e["gs"], T + U - 1)
                o = ps[3 + jj % 2][:, 0:D]
                T_.matmul(o, attrT[:, jj % 2, :], weh[:, D:2 * D], start=True, stop=False)
                T_.matmul(o, attrT[:, jj % 2, :], wel[:, D:2 * D], start=False, stop=True).then_inc(e["gp"], 1)

            def C(c, jj):
                T = c * BODY + jj
                pe.wait_ge(e["htl"], T + 3)
                pe.wait_ge(e["msg"], T + 1)
                o = ps[5 + jj % 2][:, 0:D]
                for k in range(KC):
                    for n_, (a, b) in enumerate(((HTh, w2h), (HTh, w2l), (HTl, w2h))):
                        T_.matmul(o, a[:, jj % 2, k, :], b[:, k, :], start=k == 0 and n_ == 0, stop=False)
                T_.matmul(o, ones_r[:, :], b2h[:, :], start=False, stop=True).then_inc(e["core"], 1)

            def D_(c, jj):
                T = c * BODY + jj
                pe.wait_ge(hot[2], T + 1)
                pe.wait_ge(e["ml"], T + 1 + MS)
                pe.wait_ge(done[2], T + BODY)
                T_.matmul(ps[7][:, 0:D], onehot[:, jj % U, :], mh[:, jj % MS, :], start=True, stop=False)
                T_.matmul(ps[7][:, 0:D], onehot[:, jj % U, :], ml[:, jj % MS, :], start=False, stop=True)\
                    .then_inc(summed[2], 1)

            def pe_turn(c, first=False, last=False):
                for j in range(BODY):
                    if not (last and j == BODY - 1):
                        A(c, j + 1)
                    B(c, j)
                    if not first or j >= 1:
                        C(c, j - 1)
                    if not first or j >= SUM_LAG:
                        D_(c, j - SUM_LAG)

            A(0, 0)
            pe_turn(0, first=True)
            with pe.Fori(1, TURNS - 1) as c:
                pe_turn(c)
            pe_turn(TURNS - 1, last=True)
            C(TURNS - 1, BODY - 1)
            for j in range(BODY - SUM_LAG, BODY):
                D_(TURNS - 1, j)

            for L in (3, 4):
                edge_sums(L, D)
                products(L, wab[:, L - 3], D)


_OUT = ((N, D), "float32")


def kernel(x, src, dst, edge_attr_64, edge_type_16, edge_weight1, L0_gnn_weight, L0_gnn_gate_weight,
           L1_gnn_W, L1_gnn_b, L2_gnn_W1, L2_gnn_b1, L2_gnn_W2, L2_gnn_b2, L2_gnn_Wg, L2_gnn_bg,
           L2_gnn_gamma, L2_gnn_beta, L3_gnn_W0, L3_gnn_b0, L3_gnn_g0, L3_gnn_beta0, L3_gnn_W1,
           L3_gnn_b1, L3_gnn_g1, L3_gnn_beta1):
    import numpy as np
    import concourse.bacc as bacc
    from concourse.bass_utils import run_bass_kernel_spmd

    given = [
        ("x", x), ("src", src), ("dst", dst), ("edge_attr", edge_attr_64), ("edge_type", edge_type_16),
        ("edge_weight", edge_weight1), ("w_rel", L0_gnn_weight),
        ("w_gate", np.asarray(L0_gnn_gate_weight)[:, :, 0].T), ("w_l1", np.asarray(L1_gnn_W).T), ("b_l1", L1_gnn_b),
        ("w1", L2_gnn_W1), ("b1", L2_gnn_b1), ("w2", L2_gnn_W2), ("b2", L2_gnn_b2), ("wg", L2_gnn_Wg), ("bg", L2_gnn_bg),
        ("gamma", L2_gnn_gamma), ("beta", L2_gnn_beta),
        ("w_a", np.asarray(L3_gnn_W0).T), ("b_a", L3_gnn_b0), ("g_a", L3_gnn_g0), ("be_a", L3_gnn_beta0),
        ("w_b", np.asarray(L3_gnn_W1).T), ("b_b", L3_gnn_b1), ("g_b", L3_gnn_g1), ("be_b", L3_gnn_beta1),
    ]
    edge_attr = np.asarray(edge_attr_64)
    given[3] = ("edge_attr", np.concatenate([edge_attr, np.zeros((SLOTS - E, DE), edge_attr.dtype)]))
    nc = bacc.Bacc("TRN2", target_bir_lowering=False, num_devices=1)
    arrays, args = {}, {}
    for name, a in given:
        a = np.ascontiguousarray(a)
        arrays[f"in_{name}"] = a
        args[name] = nc.dram_tensor(f"in_{name}", a.shape, mybir.dt.from_np(a.dtype), kind="ExternalInput").ap()
    args["out"] = nc.dram_tensor("out_0", _OUT[0], mybir.dt.from_np(np.dtype(_OUT[1])), kind="ExternalOutput").ap()
    program(nc, **args)
    r = run_bass_kernel_spmd(nc, [arrays], core_ids=[0])
    return r.results[0]["out_0"]
```
